# Optimizing a Trainium2 kernel written in Bass

```python
import numpy as np
import jax
import jax.numpy as jnp

def _softmax(x, axis=-1):
    return jax.nn.softmax(x, axis=axis)

def _gelu(x):
    return jax.nn.gelu(x, approximate=True)

def _silu(x):
    return jax.nn.silu(x)

def _sigmoid(x):
    return jax.nn.sigmoid(x)

def _layernorm(x, axis=-1, eps=1e-05):
    m = jnp.mean(x, axis=axis, keepdims=True)
    v = jnp.var(x, axis=axis, keepdims=True)
    return (x - m) / jnp.sqrt(v + eps)

def _scatter_add(tgt, idx, src, axis=0):
    return tgt.at[idx].add(src)

def _segment_sum(src, seg, n):
    return jax.ops.segment_sum(src, seg, n)
kernel_name = 'mk_gnn_resnorm_d2_gnn_r32_b62c65'

def setup_inputs(seed: int=0):
    np.random.seed(seed)
    _w = jnp.asarray

    def _rec_inputs():
        import jax
        import jax.numpy as jnp
        _gk = jax.random.key(seed)
        x = -0.0003713 + 1 * jax.random.normal(jax.random.fold_in(_gk, 1), (3125, 256), jnp.float32)
        src = jax.random.randint(jax.random.fold_in(_gk, 2), (50000,), 0, 3125, jnp.int32)
        dst = jax.random.randint(jax.random.fold_in(_gk, 3), (50000,), 0, 3125, jnp.int32)
        _o = jnp.argsort(dst, stable=True)
        src = src[_o]
        dst = dst[_o]
        edge_type_16 = jax.random.randint(jax.random.fold_in(_gk, 12), (50000,), 0, 16, jnp.int32)
        edge_type_5 = jax.random.randint(jax.random.fold_in(_gk, 13), (50000,), 0, 5, jnp.int32)
        edge_weight1 = jax.random.uniform(jax.random.fold_in(_gk, 14), (50000, 1), jnp.float32, 0.0, 1)
        node_type_3 = jax.random.randint(jax.random.fold_in(_gk, 15), (3125,), 0, 3, jnp.int32)
        return (x, src, dst, edge_type_16, edge_type_5, edge_weight1, node_type_3)
    x, src, dst, edge_type_16, edge_type_5, edge_weight1, node_type_3 = _rec_inputs()

    def _L0_gnn_setup():
        import jax, jax.numpy as jnp
        import numpy as np
        N_NTYPES, N_ETYPES, H, D = (3, 5, 8, 32)
        N, E, C = (50000, 9375, 256)

        def typed_linear(x, W, types, n_types):
            out = jnp.zeros((x.shape[0], W.shape[-1]), x.dtype)
            for t in range(n_types):
                out = out + jnp.where((types == t)[:, None], x @ W[t], 0.0)
            return out
        key = jax.random.key(seed)
        ks = jax.random.split(key, 13)
        s_c = 1.0 / np.sqrt(C)
        s_d = 1.0 / np.sqrt(D)
        return {'x': jax.random.normal(ks[0], (N, C), jnp.float32), 'Wk': jax.random.normal(ks[1], (N_NTYPES, C, C), jnp.float32) * s_c, 'Wq': jax.random.normal(ks[2], (N_NTYPES, C, C), jnp.float32) * s_c, 'Wv': jax.random.normal(ks[3], (N_NTYPES, C, C), jnp.float32) * s_c, 'Ratt': jax.random.normal(ks[4], (N_ETYPES, H, D, D), jnp.float32) * s_d, 'Rmsg': jax.random.normal(ks[5], (N_ETYPES, H, D, D), jnp.float32) * s_d, 'pri': jax.random.uniform(ks[6], (N_ETYPES, H), jnp.float32), 'Wa': jax.random.normal(ks[7], (N_NTYPES, C, C), jnp.float32) * s_c, 'skip': jax.random.normal(ks[8], (N_NTYPES,), jnp.float32), 'src': jax.random.randint(ks[9], (E,), 0, N), 'dst': jax.random.randint(ks[10], (E,), 0, N), 'etype': jax.random.randint(ks[11], (E,), 0, N_ETYPES), 'ntype': jax.random.randint(ks[12], (N,), 0, N_NTYPES)}
    _L0_gnn_all = _L0_gnn_setup()
    _L0_gnn_in = {k: v for k, v in _L0_gnn_all.items() if k in ('Wk', 'Wq', 'Wv', 'Ratt', 'Rmsg', 'pri', 'Wa', 'skip')}
    del _L0_gnn_all

    def _L1_gnn_setup():
        import jax, jax.numpy as jnp
        import numpy as np
        N_NODES = 50000
        N_EDGES = 25000
        NUM_RELS = 16
        FEAT = 256
        OUT = 256
        key = jax.random.key(seed)
        ks = jax.random.split(key, 7)
        h = jax.random.normal(ks[0], (N_NODES, FEAT), dtype=jnp.float32)
        norm = jax.random.uniform(ks[1], (N_EDGES, 1), dtype=jnp.float32)
        weight = jax.random.normal(ks[2], (NUM_RELS, FEAT, OUT), dtype=jnp.float32) * 0.05
        gate_weight = jax.random.normal(ks[3], (NUM_RELS, FEAT, 1), dtype=jnp.float32) * 0.05
        src = jax.random.randint(ks[4], (N_EDGES,), 0, N_NODES)
        dst = jax.random.randint(ks[5], (N_EDGES,), 0, N_NODES)
        rel_type = jax.random.randint(ks[6], (N_EDGES,), 0, NUM_RELS)
        return {'h': h, 'norm': norm, 'weight': weight, 'gate_weight': gate_weight, 'src': src, 'dst': dst, 'rel_type': rel_type}
    _L1_gnn_all = _L1_gnn_setup()
    _L1_gnn_in = {k: v for k, v in _L1_gnn_all.items() if k in ('weight', 'gate_weight')}
    del _L1_gnn_all
    return {'x': x, 'src': src, 'dst': dst, 'edge_type_16': edge_type_16, 'edge_type_5': edge_type_5, 'edge_weight1': edge_weight1, 'node_type_3': node_type_3, 'L0_gnn_Wk': _L0_gnn_in['Wk'], 'L0_gnn_Wq': _L0_gnn_in['Wq'], 'L0_gnn_Wv': _L0_gnn_in['Wv'], 'L0_gnn_Ratt': _L0_gnn_in['Ratt'], 'L0_gnn_Rmsg': _L0_gnn_in['Rmsg'], 'L0_gnn_pri': _L0_gnn_in['pri'], 'L0_gnn_Wa': _L0_gnn_in['Wa'], 'L0_gnn_skip': _L0_gnn_in['skip'], 'L1_gnn_weight': _L1_gnn_in['weight'], 'L1_gnn_gate_weight': _L1_gnn_in['gate_weight']}

def reference(x, src, dst, edge_type_16, edge_type_5, edge_weight1, node_type_3, L0_gnn_Wk, L0_gnn_Wq, L0_gnn_Wv, L0_gnn_Ratt, L0_gnn_Rmsg, L0_gnn_pri, L0_gnn_Wa, L0_gnn_skip, L1_gnn_weight, L1_gnn_gate_weight):
    import jax
    import jax.numpy as jnp

    def _L0_gnn_ref(x, Wk, Wq, Wv, Ratt, Rmsg, pri, Wa, skip, src, dst, etype, ntype):
        import jax, jax.numpy as jnp
        import numpy as np
        N_NTYPES, N_ETYPES, H, D = (3, 5, 8, 32)
        N, E, C = (50000, 9375, 256)

        def typed_linear(x, W, types, n_types):
            out = jnp.zeros((x.shape[0], W.shape[-1]), x.dtype)
            for t in range(n_types):
                out = out + jnp.where((types == t)[:, None], x @ W[t], 0.0)
            return out
        n = x.shape[0]
        k = typed_linear(x, Wk, ntype, N_NTYPES).reshape(n, H, D)
        q = typed_linear(x, Wq, ntype, N_NTYPES).reshape(n, H, D)
        v = typed_linear(x, Wv, ntype, N_NTYPES).reshape(n, H, D)
        k_e = k[src]
        v_e = v[src]
        q_e = q[dst]
        kw = jnp.zeros_like(k_e)
        mv = jnp.zeros_like(v_e)
        for r in range(N_ETYPES):
            m = (etype == r)[:, None, None]
            kw = kw + jnp.where(m, jnp.einsum('ehd,hdf->ehf', k_e, Ratt[r]), 0.0)
            mv = mv + jnp.where(m, jnp.einsum('ehd,hdf->ehf', v_e, Rmsg[r]), 0.0)
        a = (kw * q_e).sum(-1) * pri[etype] / jnp.sqrt(jnp.asarray(D, x.dtype))
        amax = jax.ops.segment_max(a, dst, num_segments=n)
        ex = jnp.exp(a - amax[dst])
        denom = jax.ops.segment_sum(ex, dst, num_segments=n)
        attn = ex / denom[dst]
        h = jax.ops.segment_sum(mv * attn[..., None], dst, num_segments=n)
        h = h.reshape(n, H * D)
        h = typed_linear(h, Wa, ntype, N_NTYPES)
        alpha = jax.nn.sigmoid(skip)[ntype][:, None]
        return h * alpha + x * (1.0 - alpha)

    def _L1_gnn_ref(h, norm, weight, gate_weight, src, dst, rel_type):
        import jax, jax.numpy as jnp
        import numpy as np
        N_NODES = 50000
        N_EDGES = 25000
        NUM_RELS = 16
        FEAT = 256
        OUT = 256
        n_nodes = h.shape[0]
        all_msg = jnp.einsum('nf,rfo->rno', h, weight)
        msg = all_msg[rel_type, src] * norm
        all_gate = jnp.einsum('nf,rf->rn', h, gate_weight[..., 0])
        gate = jax.nn.sigmoid(all_gate[rel_type, src])[:, None]
        msg = msg * gate
        agg = jax.ops.segment_sum(msg, dst, num_segments=n_nodes)
        return jax.nn.relu(agg)
    x = _layernorm(x + _L0_gnn_ref(x, L0_gnn_Wk, L0_gnn_Wq, L0_gnn_Wv, L0_gnn_Ratt, L0_gnn_Rmsg, L0_gnn_pri, L0_gnn_Wa, L0_gnn_skip, src, dst, edge_type_5, node_type_3), axis=-1)
    x = _layernorm(x + _L1_gnn_ref(x, edge_weight1, L1_gnn_weight, L1_gnn_gate_weight, src, dst, edge_type_16), axis=-1)
    return x

_drawn_inputs = setup_inputs


def setup_inputs(seed=0):
    import zlib

    import numpy as np

    out = dict(_drawn_inputs(seed))
    spreads = {}
    factors = {}
    for name, (base, spread) in spreads.items():
        noise = np.random.default_rng([zlib.crc32(name.encode()), seed]).standard_normal(out[name].shape)
        drawn = base * np.exp(spread * noise) if base else spread * noise
        out[name] = jnp.asarray(drawn.astype(out[name].dtype))
    for name, factor in factors.items():
        out[name] = (out[name] * factor).astype(out[name].dtype)
    return out
```

```python
from contextlib import ExitStack

import concourse.bass as bass
from concourse import mybir

F32 = mybir.dt.float32
I32 = mybir.dt.int32
ALU = mybir.AluOpType
ACT = mybir.ActivationFunctionType
AX = mybir.AxisListType

P = 128
C = 256
HALVES = C // P
H, D = 8, 32
NT, ET, RT = 3, 5, 16
N, E = 3125, 50000
NODES = 112
ROUNDS = -(-N // NODES)
NPAD = ROUNDS * NODES
U = 16
G, GU = 4, 4
ROUND_EDGES = P * U
EPAD = E + ROUND_EDGES
COUNT_COLS = -(-E // P)
FAR = 1 << 20
BIG = 1e30
ROW = 2 * C + H
SUPER = 4
STEPS = ROUNDS // SUPER
EPS = 1e-5
CHUNKS = RT // 2
LAST = ROUNDS // 2 - 1
STAGES = 2
FIELDS = 6


class Round:

    def __init__(self, eng, i, par):
        self.eng, self.i, self.par = eng, i, par
        self.number = 2 * i + par
        self.done = 2 * i + (par + 1)
        self.before = 2 * i + (par - 1)
        self.first = isinstance(i, int) and self.number == 0
        self.final = isinstance(i, int) and self.number == ROUNDS - 1

    def loads(self, n):
        return self.i * (16 * n) + 16 * n

    def stores_before(self):
        return self.i * 32 + 16 * self.par

    def last(self):
        return Round(self.eng, self.i, 0) if self.par else Round(self.eng, self.i - 1, 1)

    def next(self):
        return Round(self.eng, self.i, 1) if self.par == 0 else Round(self.eng, self.i + 1, 0)


def settle(eng, sem):
    eng.wait_ge(sem, 1)


def wait(eng, sem, value):
    if not (isinstance(value, int) and value <= 0):
        eng.wait_ge(sem, value)


def build(nc, x, nt_rows, rec, norm, dst_grid, Wk, Wq, Wv, Ratt, Rmsg, pri, Wa, skip, Wr, gate_w, out):
    ktab = nc.dram_tensor("kv_table", [NPAD * ET, 2 * C], F32).ap()
    qtab = nc.dram_tensor("query_table", [NPAD, C], F32).ap()
    x1tab = nc.dram_tensor("x1_table", [NPAD, C], F32).ap()
    mtab = nc.dram_tensor("message_table", [NPAD * RT, C], F32).ap()
    ktab_n = ktab.rearrange("(n r) c -> n (r c)", r=ET)
    mtab_n = mtab.rearrange("(n r) c -> n (r c)", r=RT)

    ctx = ExitStack()
    with ctx:
        def sb(name, shape, dt=F32):
            return ctx.enter_context(nc.sbuf_tensor(name, shape, dt))

        def sem(name):
            return ctx.enter_context(nc.semaphore(name))

        def sems(name, n):
            return [sem(f"{name}{k}") for k in range(n)]

        arena = sb("arena", [P, 2 * U * ROW])
        kv = arena[:, :].rearrange("p (b u c) -> p b u c", b=2, u=U)
        a0 = ROUNDS * C
        x_all = arena[:NODES, 0:a0].rearrange("p (j c) -> p j c", j=ROUNDS)
        wsz = NT * HALVES * C
        w_in = [arena[:, a0 + k * wsz:a0 + (k + 1) * wsz].rearrange("p (t h n) -> p t h n", t=NT, h=HALVES)
                for k in range(3)]
        a1 = a0 + 3 * wsz
        SN = SUPER * NODES
        xmT = arena[:, a1:a1 + NT * HALVES * SN].rearrange("p (t h n) -> p t h n", t=NT, h=HALVES)
        a2 = a1 + NT * HALVES * SN
        kvT = arena[:, a2:a2 + 4 * SN].rearrange("p (k h n) -> p k h n", k=2, h=HALVES)
        assert a2 + 4 * SN <= 2 * U * ROW

        wr = sb("wr", [P, HALVES, RT, C])
        mstage = sb("mstage", [P, STAGES, RT // STAGES, C])
        rel = mstage[:, :, :, :].rearrange("p a b c -> p (a b c)")[:, 0:2 * HALVES * ET * P].rearrange(
            "p (k h r n) -> p k h r n", k=2, h=HALVES, r=ET)
        wa = sb("wa", [P, NT, HALVES, C])
        onehot = sb("onehot", [P, 2, U, NODES])
        xm = onehot[:, :, :, :].rearrange("p a b c -> p (a b c)")[:NODES, 0:NT * SUPER * C].rearrange(
            "p (t s c) -> p t s c", t=NT, s=SUPER)
        onehotT = sb("onehotT", [P, U, P])
        tstage = sb("tstage", [P, 2, ET, 2 * C])
        qstage = sb("qstage", [P, SUPER, C])
        recs = sb("recs", [P, ROUNDS, U, FIELDS], I32)
        norms = sb("norms", [P, ROUNDS, U])
        dstl = sb("dstl", [P, ROUNDS, U])
        edge_mask = sb("edge_mask", [P, ROUNDS, 2, U])
        reach = sb("reach", [P, ROUNDS, 2, U])
        cell = sb("cell", [P, 2, ROUNDS, U])
        ends = sb("ends", [P, ROUNDS, 2])
        cgrid = onehotT[:, :, :].rearrange("p a b -> p (a b)")
        grid_i = cgrid[:, 0:COUNT_COLS].bitcast(I32)
        grid_f = cgrid[:, COUNT_COLS:2 * COUNT_COLS]
        grid_o = cgrid[:, 2 * COUNT_COLS:3 * COUNT_COLS]
        same = cgrid[:, 1024:1024 + 2 * ROUNDS * U].rearrange("p (j k u) -> p j k u", j=ROUNDS, k=2)
        cnt = sb("cnt", [P, ROUNDS])
        starts = sb("starts", [1, ROUNDS], I32)
        ones = sb("ones", [P, 1])
        ident = sb("ident", [P, P])
        iota_n = sb("iota_n", [P, NODES])
        base = sb("base", [P, ROUNDS])
        nt_i = sb("nt_i", [P, ROUNDS], I32)
        nmask = sb("nmask", [P, ROUNDS, NT])
        calpha = sb("calpha", [P, ROUNDS, NT])
        keep = sb("keep", [P, ROUNDS])
        skips = sb("skips", [P, NT])
        alpha = sb("alpha", [P, NT])
        pris = sb("pris", [P, HALVES, ET])
        gw = sb("gw", [P, HALVES, RT])
        eps = sb("eps", [P, 1])
        idx = sb("idx", [P, 2, U], I32)
        qb = sb("qb", [P, 2, C])
        xb = sb("xb", [P, 2, C])
        S = sb("S", [P, H, U])
        masks = sb("masks", [P, 2, H, U])
        FB = sb("FB", [P, 2, H, U])
        gsum = sb("gsum", [P, 2, H])
        carry_in = sb("carry_in", [H, 4, P])
        carry = sb("carry", [H, 2, P + 1])
        m2 = sb("m2", [P, 2, H, U])
        mx = sb("mx", [P, H, U])
        dd = sb("dd", [P, H, U])
        den = sb("den", [P, H])
        rden = sb("rden", [P, H])
        after = tstage[:, :, :, :].rearrange("p b r c -> p (b r c)")
        hN, xs, z = (after[:, k * C:(k + 1) * C] for k in range(3))
        hm = after[:, 3 * C:(3 + NT) * C].rearrange("p (t c) -> p t c", t=NT)
        hmT = after[:, 6 * C:6 * C + HALVES * NT * NODES].rearrange("p (h t n) -> p h t n", h=HALVES, t=NT)
        st6 = sb("st6", [P, 6])
        mv = sb("mv", [P, 2])
        sd = sb("sd", [P, 1])
        rstd = sb("rstd", [P, 1])
        x1 = sb("x1", [P, 2, C])
        x1T = sb("x1T", [P, HALVES, NODES])
        eg = sb("eg", [P, RT])
        eg1 = sb("eg1", [P, RT])
        gate = sb("gate", [P, RT])

        bank = [ctx.enter_context(nc.psum_tensor(f"bank{k}", [P, 512], F32)) for k in range(8)]
        b_qe, b_ohT, b_agg, b_tmp, b_out, b_m = bank[0:2], bank[2], bank[3], bank[4], bank[5], bank[6:8]

        ld_grid, ld_x, ld_w, ld_wr, ld_rel, ld_small, ld_rec = (sem(n) for n in (
            "ld_grid", "ld_x", "ld_w", "ld_wr", "ld_rel", "ld_small", "ld_rec"))
        const_ready, zeroed, rel_ready = sem("const_ready"), sem("zeroed"), sem("rel_ready")
        pool_step = sem("pool_step")
        counted = sem("counted")
        alpha_exp, grid_ready, meta_step = sem("alpha_exp"), sem("grid_ready"), sem("meta_step")
        cnt_summed, starts_ready, meta_ready, mask_ready = (sem(n) for n in (
            "cnt_summed", "starts_ready", "meta_ready", "mask_ready"))
        xm_ready, xm_used, t_filled, t_act, t_dve = (sem(n) for n in (
            "xm_ready", "xm_used", "t_filled", "t_act", "t_dve"))
        t_stored, q_stored = sems("t_stored", 2), sems("q_stored", 2)

        q_loaded, x_loaded = sems("q_loaded", 2), sems("x_loaded", 2)
        idx_ready, oh_ready = sems("idx_ready", 2), sem("oh_ready")
        kv_landed = [sems(f"kv_landed{p}_", G) for p in range(2)]
        ohT_filled, ohT_ready = sems("ohT_filled", G), sems("ohT_ready", G)
        qe_ready, qe_used = sems("qe_ready", U // 2), sems("qe_used", U // 2)
        prod, scored = sems("prod", G), sems("scored", G)
        masks_ready, scanned, carryT, carry_copied = (sem(n) for n in (
            "masks_ready", "scanned", "carryT", "carry_copied"))
        carried, backT, m_a, m_b, m_c, d_ready, ex_ready = (sem(n) for n in (
            "carried", "backT", "m_a", "m_b", "m_c", "d_ready", "ex_ready"))
        weighted = sems("weighted", G)
        agg_done = sem("agg_done")
        den_ready, rden_ready, hN_ready, hm_ready = (sem(n) for n in (
            "den_ready", "rden_ready", "hN_ready", "hm_ready"))
        hT_filled, hT_ready = sems("hT_filled", HALVES), sems("hT_ready", HALVES)
        wa_done, xs_ready, z_ready, st_ready, mv_ready, sd_ready, rstd_ready, x1_ready = (sem(n) for n in (
            "wa_done", "xs_ready", "z_ready", "st_ready", "mv_ready", "sd_ready", "rstd_ready", "x1_ready"))
        x1T_filled, x1T_ready, gate_psum, eg_ready, eg1_ready, gate_ready = (sem(n) for n in (
            "x1T_filled", "x1T_ready", "gate_psum", "eg_ready", "eg1_ready", "gate_ready"))
        m_filled, m_evac = sems("m_filled", CHUNKS), sems("m_evac", CHUNKS)
        m_stored = sems("m_stored", STAGES)
        x1_stored = sem("x1_stored")

        l_idx, l_oh0, l_oh, l_agg = sems("l_idx", 2), sem("l_oh0"), sem("l_oh"), sem("l_agg")
        l_landed = [sems(f"l_landed{p}_", G) for p in range(2)]
        l_x = sems("l_x", 2)
        l_z, l_st, l_mv, l_sd, l_rstd, l_y = (sem(n) for n in (
            "l_z", "l_st", "l_mv", "l_sd", "l_rstd", "l_y"))
        l_out = sem("l_out")

        block = ctx.enter_context(nc.Block())

        JOBS = ([("xT", t, h) for t in range(NT) for h in range(HALVES)]
                + [("kvT", k, h) for k in range(2) for h in range(HALVES)]
                + [("q", s) for s in range(SUPER)]
                + [("tab", s, q) for s in range(SUPER) for q in range(5)])
        NJ = len(JOBS)

        def on_act(k):
            return JOBS[k][0] in ("xT", "q") or (JOBS[k][0] == "tab" and (JOBS[k][1] + JOBS[k][2]) % 2 == 0)
        A_IDX, D_IDX = {}, {}
        for k in range(NJ):
            d_ = A_IDX if on_act(k) else D_IDX
            d_[k] = len(d_) + 1
        NA, ND = len(A_IDX), len(D_IDX)

        def rounds(eng, body):
            for par in range(2):
                body(Round(eng, 0, par))
            with eng.Fori(1, LAST) as i:
                for par in range(2):
                    body(Round(eng, i, par))
            for par in range(2):
                body(Round(eng, LAST, par))

        def table_part(eng, s, job, b):
            _, t, q = job
            st = tstage[:NODES, t % 2, :, :]
            eng.wait_ge(t_stored[t % 2], s * 32 + 16 * (t // 2))
            if q < 4:
                return st[:, 0:4, q * P:(q + 1) * P], b[:NODES, :].rearrange("p (r n) -> p r n", r=4)
            return st[:, 4, :], b[:NODES, :]

        @block.sync
        def _(sp):
            for k in range(2):
                sp.sem_inc(t_stored[k], 32)
                sp.sem_inc(q_stored[k], 32)
            sp.dma_start(grid_i, dst_grid).then_inc(ld_grid, 16)
            sp.dma_start(x_all, x.rearrange("(j p) c -> p j c", p=NODES)).then_inc(ld_x, 16)
            for k, w in enumerate((Wk, Wv, Wq)):
                sp.dma_start(w_in[k], w.rearrange("t (h p) n -> p t h n", p=P)).then_inc(ld_w, 16)
            sp.wait_ge(zeroed, 1)
            for k, r in enumerate((Ratt, Rmsg)):
                for h in range(H):
                    q = D * (h % 4)
                    sp.dma_start(rel[q:q + D, k, h // 4, :, q:q + D],
                                 r[:, h].rearrange("r d f -> d r f")).then_inc(ld_rel, 16)
            for h in range(H):
                q = D * (h % 4)
                sp.dma_start(pris[q:q + D, h // 4, :], pri[h:h + 1, :].to_broadcast([D, ET])).then_inc(ld_rel, 16)
            sp.wait_ge(starts_ready, 1)
            with sp.Fori(0, ROUNDS) as j:
                s = sp.value_load(starts[0:1, bass.ds(j, 1)], min_val=0, max_val=E)
                sp.dma_start(recs[:, bass.ds(j, 1), :, :].rearrange("p j u f -> p (j u f)"),
                             rec[bass.ds(s, ROUND_EDGES), :].rearrange("(p u) f -> p (u f)", p=P)).then_inc(ld_rec, 16)
                sp.dma_start(norms[:, bass.ds(j, 1), :].rearrange("p j u -> p (j u)"),
                             norm[bass.ds(s, ROUND_EDGES)].rearrange("(p u) -> p u", p=P)).then_inc(ld_rec, 16)
            with sp.Fori(1, STEPS + 1) as s:
                for t in range(SUPER):
                    ks = [JOBS.index(("tab", t, q)) for q in range(5)]
                    sp.wait_ge(t_act, s * NA + max(A_IDX[k] for k in ks if k in A_IDX))
                    sp.dma_start(qtab[bass.ds(s * SN + (t - SUPER) * NODES, NODES), :], qstage[:NODES, t, :]).then_inc(q_stored[t % 2], 16)
                    sp.wait_ge(t_dve, s * ND + max(D_IDX[k] for k in ks if k in D_IDX))
                    sp.dma_start(ktab_n[bass.ds(s * SN + (t - SUPER) * NODES, NODES), :],
                                 tstage[:NODES, t % 2, :, :].rearrange("p r c -> p (r c)")).then_inc(t_stored[t % 2], 16)
            for k in range(2):
                sp.wait_ge(q_stored[k], 16 * (ROUNDS // 2 + 2))

            def load(r):
                wait(sp, qe_used[U // 2 - 1], r.before)
                sp.dma_start(qb[:NODES, r.par, :], qtab[bass.ds(r.number * NODES, NODES), :]).then_inc(q_loaded[r.par], 16)
                wait(sp, xs_ready, r.before)
                sp.dma_start(xb[:NODES, r.par, :], x[bass.ds(r.number * NODES, NODES), :]).then_inc(x_loaded[r.par], 16)

            def store(f):
                sp.wait_ge(x1_ready, f.done)
                sp.dma_start(x1tab[bass.ds(f.number * NODES, NODES), :], x1[:NODES, f.par, :]).then_inc(x1_stored, 16)
                for b in range(STAGES):
                    sp.wait_ge(m_evac[(b + 1) * CHUNKS // STAGES - 1], f.done)
                    w = RT // STAGES * C
                    sp.dma_start(mtab_n[bass.ds(f.number * NODES, NODES), b * w:(b + 1) * w],
                                 mstage[:NODES, b, :, :].rearrange("p r c -> p (r c)")).then_inc(m_stored[b], 16)

            def l0(r):
                if not r.final:
                    load(r.next())
                if not r.first:
                    store(r.last())
            load(Round(sp, 0, 0))
            rounds(sp, l0)
            store(Round(sp, LAST, 1))
            sp.wait_ge(x1_stored, 16 * ROUNDS)

            def l1(r):
                wait(sp, l_z, r.before)
                sp.dma_start(xb[:NODES, r.par, :], x1tab[bass.ds(r.number * NODES, NODES), :]).then_inc(l_x[r.par], 16)
                if not r.first:
                    last(r.last())

            def last(f):
                sp.wait_ge(l_y, f.done)
                sp.dma_start(out[bass.ds(f.number * NODES, NODES), :], x1[:NODES, f.par, :]).then_inc(l_out, 16)
            rounds(sp, l1)
            last(Round(sp, LAST, 1))
            sp.wait_ge(l_out, 16 * ROUNDS)

        @block.gpsimd
        def _(pool):
            pool.memset(mstage[:, :, :, :], 0.0).then_inc(zeroed, 1)
            pool.memset(ident[:, :], 0.0).then_inc(pool_step, 1)
            pool.memset(ones[:, :], 1.0)
            pool.memset(eps[:, :], EPS)
            pool.memset(carry[:, 0, 0:1], -BIG)
            pool.memset(carry[:, 1, P:P + 1], -BIG)
            pool.memset(cell[:, :, :, :], 0.0).then_inc(pool_step, 1)
            pool.iota(iota_n[:, :], pattern=[[1, NODES]], base=0, channel_multiplier=0,
                      allow_small_or_imprecise_dtypes=True)
            pool.iota(base[:, :], pattern=[[NODES, ROUNDS]], base=0, channel_multiplier=0,
                      allow_small_or_imprecise_dtypes=True)
            pool.wait_ge(pool_step, 2)
            pool.memset(cell[:, 0, :, 0:1], 2 * BIG)
            pool.memset(cell[:, 1, :, U - 1:U], 2 * BIG)
            pool.affine_select(out=ident[:, :], in_=ident[:, :], compare_op=ALU.not_equal, fill=1.0,
                               base=0, pattern=[[-1, P]], channel_multiplier=1).then_inc(const_ready, 1)
            pool.dma_start(nt_i[:NODES, :], nt_rows).then_inc(ld_small, 16)
            pool.dma_start(skips[:, :], skip.rearrange("(a t) -> a t", a=1).to_broadcast([P, NT])).then_inc(ld_small, 16)
            pool.dma_start(gw[:, :, :], gate_w.rearrange("(h p) r -> p h r", p=P)).then_inc(ld_wr, 16)
            pool.dma_start(wa[:, :, :, :], Wa.rearrange("t (h p) n -> p t h n", p=P)).then_inc(ld_wr, 16)
            for h in range(HALVES):
                pool.dma_start(wr[:, h, :, :], Wr[:, h * P:(h + 1) * P, :].rearrange("r p n -> p r n")).then_inc(ld_wr, 16)

            for k in range(2):
                pool.wait_ge(t_stored[k], 16 * (ROUNDS // 2 + 2))

            def gather(pair, table, width, indices, landed):
                for par in range(2):
                    settle(pool, const_ready)
                    pool.wait_ge(indices[par], pair)
                    for u in range(U):
                        pool.indirect_dma_start(kv[:, par, u, 0:width], None, table,
                                                bass.IndirectOffsetOnAxis(ap=idx[:, par, u:u + 1], axis=0)
                                                ).then_inc(landed[par][u // GU], 16)

            with pool.Fori(1, ROUNDS // 2 + 1) as pair:
                gather(pair, ktab, 2 * C, idx_ready, kv_landed)
            for b in range(STAGES):
                pool.wait_ge(m_stored[b], 16 * ROUNDS)
            pool.wait_ge(agg_done, ROUNDS)

            with pool.Fori(1, ROUNDS // 2 + 1) as pair:
                gather(pair, mtab, C, l_idx, l_landed)

        @block.tensor
        def _(pe):
            mm = nc.tensor.matmul
            pe.sem_inc(t_filled, NJ)
            pe.sem_inc(xm_used, 1)
            pe.wait_ge(const_ready, 1)
            pe.wait_ge(counted, ROUNDS)
            mm(bank[0][0:1, 0:ROUNDS], ones[:, :], cnt[:, :], start=True, stop=True).then_inc(cnt_summed, 1)
            pe.wait_ge(starts_ready, 1)
            pe.wait_ge(ld_w, 48)
            pe.wait_ge(rel_ready, 2)

            with pe.Fori(1, STEPS + 1) as s:
                pe.wait_ge(t_act, s * NA)
                pe.wait_ge(t_dve, s * ND)
                pe.wait_ge(xm_ready, s)
                for k, job in enumerate(JOBS):
                    b = bank[k % 8]
                    if k >= 8:
                        if on_act(k - 8):
                            pe.wait_ge(t_act, s * NA + A_IDX[k - 8])
                        else:
                            pe.wait_ge(t_dve, s * ND + D_IDX[k - 8])
                    if job[0] == "xT":
                        _, t, h = job
                        for q in range(SUPER):
                            last = nc.tensor.transpose(b[:, q * NODES:(q + 1) * NODES],
                                                       xm[:, t, q, h * P:(h + 1) * P], ident[:NODES, :NODES])
                    elif job[0] == "kvT":
                        _, kk, ho = job
                        if (kk, ho) == (0, 0):
                            pe.wait_ge(t_act, s * NA + 6)
                        for n, (t, h) in enumerate((t, h) for t in range(NT) for h in range(HALVES)):
                            last = mm(b[:, 0:SN], w_in[kk][:, t, h, ho * P:(ho + 1) * P], xmT[:, t, h, :],
                                      start=(n == 0), stop=(n == 2 * NT - 1))
                            if (kk, ho, n) == (0, 0, 0):
                                last.then_inc(xm_used, 1)
                    elif job[0] == "q":
                        for n, (t, h) in enumerate((t, h) for t in range(NT) for h in range(HALVES)):
                            c = job[1] * NODES
                            last = mm(b[:NODES, 0:C], xmT[:, t, h, c:c + NODES], w_in[2][:, t, h, :],
                                      start=(n == 0), stop=(n == 2 * NT - 1))
                    else:
                        _, t, q = job
                        c = t * NODES
                        if (t, q) == (0, 0):
                            pe.wait_ge(t_dve, s * ND + 4)
                        if q < 4:
                            kk, h = q // 2, q % 2
                            last = mm(b[:NODES, 0:4 * P], kvT[:, kk, h, c:c + NODES], rel[:, kk, h, 0:4, :],
                                      start=True, stop=True)
                        else:
                            for kk in range(2):
                                for h in range(2):
                                    o = (2 * kk + h) * P
                                    last = mm(b[:NODES, o:o + P], kvT[:, kk, h, c:c + NODES], rel[:, kk, h, 4, :],
                                              start=True, stop=True)
                    last.then_inc(t_filled, 1)
            pe.wait_ge(t_act, (STEPS + 1) * NA)
            pe.wait_ge(t_dve, (STEPS + 1) * ND)
            pe.wait_ge(ld_wr, 64)

            def turn_onehot(r, g):
                if g == 0:
                    pe.wait_ge(oh_ready, r.done)
                if g:
                    pe.wait_ge(ohT_ready[g - 1], r.done)
                else:
                    wait(pe, ohT_ready[G - 1], r.number)
                for q in range(GU):
                    last = nc.tensor.transpose(b_ohT[:NODES, q * P:(q + 1) * P],
                                               onehot[:, r.par, g * GU + q, :], ident[:, :])
                last.then_inc(ohT_filled[g], 1)

            def hand_queries(r, g):
                if g == 0:
                    pe.wait_ge(q_loaded[r.par], r.loads(1))
                pe.wait_ge(ohT_ready[g], r.done)
                for pr in range(2 * g, 2 * g + 2):
                    if pr >= 2:
                        pe.wait_ge(qe_used[pr - 2], r.done)
                    else:
                        wait(pe, qe_used[U // 2 - 2 + pr], r.number)
                    for q in range(2):
                        last = mm(b_qe[pr % 2][:, q * C:(q + 1) * C], onehotT[:NODES, 2 * pr + q, :],
                                  qb[:NODES, r.par, :], start=True, stop=True)
                    last.then_inc(qe_ready[pr], 1)

            def turn_h(f):
                pe.wait_ge(hm_ready, f.done)
                for h in range(HALVES):
                    wait(pe, m_evac[CHUNKS - 2 + h], f.number)
                    for t in range(NT):
                        last = nc.tensor.transpose(b_m[h][:, t * NODES:(t + 1) * NODES],
                                                   hm[:NODES, t, h * P:(h + 1) * P], ident[:NODES, :NODES])
                    last.then_inc(hT_filled[h], 1)

            def project(f):
                for h in range(HALVES):
                    pe.wait_ge(hT_ready[h], f.done)
                for n, (h, t) in enumerate((h, t) for h in range(HALVES) for t in range(NT)):
                    last = mm(b_out[:NODES, 0:C], hmT[:, h, t, :], wa[:, t, h, :],
                              start=(n == 0), stop=(n == 2 * NT - 1))
                last.then_inc(wa_done, 1)

            def turn_x1(f):
                pe.wait_ge(x1_ready, f.done)
                for h in range(HALVES):
                    last = nc.tensor.transpose(b_tmp[:, h * NODES:(h + 1) * NODES],
                                               x1[:NODES, f.par, h * P:(h + 1) * P], ident[:NODES, :NODES])
                last.then_inc(x1T_filled, 1)

            def gates(f):
                pe.wait_ge(x1T_ready, f.done)
                for h in range(HALVES):
                    last = mm(b_out[:NODES, C:C + RT], x1T[:, h, :], gw[:, h, :], start=(h == 0), stop=(h == 1))
                last.then_inc(gate_psum, 1)

            def message(f, c):
                if c >= 2:
                    pe.wait_ge(m_evac[c - 2], f.done)
                for h in range(HALVES):
                    last = mm(b_m[c % 2][:NODES, :], x1T[:, h, :], wr[:, h, 2 * c:2 * c + 2, :],
                              start=(h == 0), stop=(h == 1))
                last.then_inc(m_filled[c], 1)

            def turn_carry(r):
                pe.wait_ge(scanned, r.done)
                pe.wait_ge(masks_ready, r.done)
                for k, a in enumerate((FB[:, 0, :, U - 1], gsum[:, 0, :], FB[:, 1, :, 0], gsum[:, 1, :])):
                    last = nc.tensor.transpose(b_tmp[:H, k * P:(k + 1) * P], a, ident[:, :])
                last.then_inc(carryT, 1)

            def turn_back(r):
                settle(pe, const_ready)
                pe.wait_ge(carried, r.done)
                nc.tensor.transpose(b_out[:, C + RT:C + RT + H], carry[:, 0, 0:P], ident[:H, :H])
                nc.tensor.transpose(b_out[:, C + RT + H:C + RT + 2 * H], carry[:, 1, 1:P + 1],
                                    ident[:H, :H]).then_inc(backT, 1)

            def aggregate(r, g):
                pe.wait_ge(weighted[g], r.done)
                if g == 0:
                    wait(pe, hN_ready, r.number)
                for u in range(g * GU, g * GU + GU):
                    last = mm(b_agg[:NODES, 0:C + H], onehot[:, r.par, u, :], kv[:, r.par, u, C:ROW],
                              start=(u == 0), stop=(u == U - 1))
                if g == G - 1:
                    last.then_inc(agg_done, 1)

            def prepare(r):
                turn_onehot(r, 0)
                turn_onehot(r, 1)
                hand_queries(r, 0)

            def l0(r):
                f = None if r.first else r.last()
                turn_onehot(r, 2)
                hand_queries(r, 1)
                if f:
                    turn_h(f)
                turn_onehot(r, 3)
                hand_queries(r, 2)
                if f:
                    project(f)
                hand_queries(r, 3)
                if f:
                    turn_x1(f)
                    gates(f)
                    message(f, 0)
                    message(f, 1)
                turn_carry(r)
                turn_back(r)
                if not r.final:
                    prepare(r.next())
                for g in range(G):
                    if f:
                        message(f, 2 + g)
                    aggregate(r, g)
                if f:
                    message(f, 6)
                    message(f, 7)

            prepare(Round(pe, 0, 0))
            rounds(pe, l0)
            f = Round(pe, LAST, 1)
            turn_h(f)
            project(f)
            turn_x1(f)
            gates(f)
            for c in range(CHUNKS):
                message(f, c)

            def l1(r):
                wait(pe, l_z, r.before)
                pe.wait_ge(l_oh, r.done)
                for u in range(U):
                    if u % GU == 0:
                        pe.wait_ge(l_landed[r.par][u // GU], r.loads(GU))
                    last = mm(bank[r.par][:NODES, 0:C], onehot[:, r.par, u, :], kv[:, r.par, u, 0:C],
                              start=(u == 0), stop=(u == U - 1))
                last.then_inc(l_agg, 1)
            wait(pe, qe_used[U // 2 - 1], ROUNDS)
            rounds(pe, l1)

        @block.scalar
        def _(act):
            a = nc.scalar.activation
            act.sem_inc(t_act, NA)
            act.wait_ge(ld_small, 32)
            a(alpha[:, :], skips[:, :], ACT.Exp, scale=-1.0).then_inc(alpha_exp, 1)
            with act.Fori(1, STEPS + 1) as s:
                for k, job in enumerate(JOBS):
                    if not on_act(k):
                        continue
                    act.wait_ge(t_filled, s * NJ + (k + 1))
                    b = bank[k % 8]
                    if job[0] == "xT":
                        o, i = xmT[:, job[1], job[2], :], b[:, 0:SN]
                    elif job[0] == "q":
                        t = job[1]
                        act.wait_ge(q_stored[t % 2], s * 32)
                        o, i = qstage[:NODES, t, :], b[:NODES, 0:C]
                    else:
                        o, i = table_part(act, s, job, b)
                    a(o, i, ACT.Copy).then_inc(t_act, 1)

            def spread_masks(r):
                wait(act, backT, r.number)
                j = bass.ds(r.number, 1)
                a(masks[:, :, :, :], edge_mask[:, j, :, :].rearrange("p j k u -> p (j k) u").unsqueeze(2)
                  .broadcast_to([P, 2, H, U]), ACT.Copy)
                a(gsum[:, :, :], ends[:, j, :].rearrange("p j k -> p (j k)").unsqueeze(2)
                  .broadcast_to([P, 2, H]), ACT.Copy).then_inc(masks_ready, 1)

            def keep_onehotT(r, g):
                act.wait_ge(ohT_filled[g], r.done)
                a(onehotT[:NODES, g * GU:(g + 1) * GU, :], b_ohT[:NODES, :].rearrange("p (a b) -> p a b", a=GU),
                  ACT.Copy).then_inc(ohT_ready[g], 1)

            def keep_hT(f):
                for h in range(HALVES):
                    act.wait_ge(hT_filled[h], f.done)
                    a(hmT[:, h, :, :], b_m[h][:, 0:NT * NODES].rearrange("p (t n) -> p t n", t=NT),
                      ACT.Copy).then_inc(hT_ready[h], 1)

            def residual(f):
                act.wait_ge(x_loaded[f.par], f.loads(1))
                wait(act, z_ready, f.number)
                a(xs[:NODES, :], xb[:NODES, f.par, :], ACT.Copy,
                  scale=keep[:NODES, bass.ds(f.number, 1)]).then_inc(xs_ready, 1)

            def deviation(f):
                act.wait_ge(mv_ready, f.done)
                a(sd[:NODES, :], mv[:NODES, 1:2], ACT.Sqrt, bias=eps[:NODES, :]).then_inc(sd_ready, 1)

            def keep_x1T(f):
                act.wait_ge(x1T_filled, f.done)
                a(x1T[:, :, :], b_tmp[:, 0:C - 2 * (P - NODES)].rearrange("p (h n) -> p h n", h=HALVES),
                  ACT.Copy).then_inc(x1T_ready, 1)
                act.wait_ge(gate_psum, f.done)
                a(eg[:NODES, :], b_out[:NODES, C:C + RT], ACT.Exp, scale=-1.0).then_inc(eg_ready, 1)

            def keep_message(f, c):
                b = c * STAGES // CHUNKS
                if c == 0:
                    act.wait_ge(gate_ready, f.done)
                if c % (CHUNKS // STAGES) == 0:
                    wait(act, m_stored[b], f.stores_before())
                act.wait_ge(m_filled[c], f.done)
                for k in range(2):
                    q = 2 * c + k
                    last = a(mstage[:NODES, b, q % (RT // STAGES), :], b_m[c % 2][:NODES, k * C:(k + 1) * C],
                             ACT.Copy, scale=gate[:NODES, q:q + 1])
                last.then_inc(m_evac[c], 1)

            def keep_carry(r):
                act.wait_ge(carryT, r.done)
                a(carry_in[:, :, :], b_tmp[:H, :].rearrange("p (k n) -> p k n", k=4), ACT.Copy).then_inc(carry_copied, 1)

            def exps(r):
                act.wait_ge(d_ready, r.done)
                a(kv[:, r.par, :, 2 * C:ROW], dd[:, :, :].rearrange("p h u -> p u h"), ACT.Exp).then_inc(ex_ready, 1)

            act.wait_ge(meta_ready, 1)
            act.wait_ge(mask_ready, 1)

            def prepare(r):
                keep_onehotT(r, 0)
                keep_onehotT(r, 1)

            def l0(r):
                f = None if r.first else r.last()
                spread_masks(r)
                keep_onehotT(r, 2)
                if f:
                    keep_hT(f)
                keep_onehotT(r, 3)
                if f:
                    residual(f)
                    deviation(f)
                    keep_x1T(f)
                    keep_message(f, 0)
                    keep_message(f, 1)
                keep_carry(r)
                exps(r)
                if not r.final:
                    prepare(r.next())
                if f:
                    for c in range(2, CHUNKS):
                        keep_message(f, c)
            prepare(Round(act, 0, 0))
            rounds(act, l0)
            f = Round(act, LAST, 1)
            keep_hT(f)
            residual(f)
            deviation(f)
            keep_x1T(f)
            for c in range(CHUNKS):
                keep_message(f, c)

            def l1(f):
                act.wait_ge(l_mv, f.done)
                a(sd[:NODES, :], mv[:NODES, 1:2], ACT.Sqrt, bias=eps[:NODES, :]).then_inc(l_sd, 1)
            rounds(act, l1)

        @block.vector
        def _(dve):
            v = nc.vector
            dve.sem_inc(t_dve, ND)
            dve.wait_ge(ld_grid, 16)
            v.tensor_copy(grid_f, grid_i).then_inc(grid_ready, 1)
            dve.wait_ge(grid_ready, 1)
            for j in range(ROUNDS):
                v.tensor_scalar(grid_o, grid_f, float(j * NODES), None, ALU.is_lt, ALU.add,
                                accum_out=cnt[:, j:j + 1]).then_inc(counted, 1)
                dve.wait_ge(counted, j + 1)
            dve.wait_ge(cnt_summed, 1)
            v.tensor_copy(starts[:, :], bank[0][0:1, 0:ROUNDS]).then_inc(starts_ready, 1)

            step = [0]

            def link(ins):
                step[0] += 1
                ins.then_inc(meta_step, 1)
                dve.wait_ge(meta_step, step[0])

            dve.wait_ge(ld_small, 32)
            dve.wait_ge(alpha_exp, 1)
            for t in range(NT):
                link(v.tensor_scalar(nmask[:NODES, :, t], nt_i[:NODES, :], float(t), None, ALU.is_equal))
            link(v.tensor_scalar_add(alpha[:, :], alpha[:, :], 1.0))
            link(v.reciprocal(alpha[:, :], alpha[:, :]))
            for t in range(NT):
                link(v.tensor_scalar(calpha[:NODES, :, t], nmask[:NODES, :, t], alpha[:NODES, t:t + 1], None, ALU.mult))
            link(v.tensor_reduce(keep[:NODES, :], calpha[:NODES, :, :], AX.X, ALU.add))
            v.tensor_scalar(keep[:NODES, :], keep[:NODES, :], -1.0, 2.0, ALU.mult, ALU.add).then_inc(mask_ready, 1)

            dve.wait_ge(ld_rel, 24 * 16)
            for h in range(HALVES):
                v.scalar_tensor_tensor(rel[:, 0, h, :, :], rel[:, 0, h, :, :], float(D) ** -0.5,
                                       pris[:, h, :].unsqueeze(2).broadcast_to([P, ET, P]),
                                       ALU.mult, ALU.mult).then_inc(rel_ready, 1)
            dve.wait_ge(ld_x, 16)
            with dve.Fori(1, STEPS + 1) as s:
                dve.wait_ge(xm_used, s)
                for t in range(NT):
                    for q in range(SUPER):
                        j = bass.ds(s * SUPER + (q - SUPER), 1)
                        last = v.tensor_scalar(xm[:, t, q, :], x_all[:, j, :].rearrange("p j c -> p (j c)"),
                                               nmask[:NODES, j, t], None, ALU.mult)
                last.then_inc(xm_ready, 1)
                for k, job in enumerate(JOBS):
                    if on_act(k):
                        continue
                    dve.wait_ge(t_filled, s * NJ + (k + 1))
                    b = bank[k % 8]
                    if job[0] == "kvT":
                        o, i = kvT[:, job[1], job[2], :], b[:, 0:SN]
                    else:
                        o, i = table_part(dve, s, job, b)
                    v.tensor_copy(o, i).then_inc(t_dve, 1)

            dve.wait_ge(ld_rec, 32 * ROUNDS)
            dve.wait_ge(const_ready, 1)
            field = lambda k: recs[:, :, :, k]
            link(v.tensor_tensor(dstl[:, :, :], field(3), base[:, :].unsqueeze(2).broadcast_to([P, ROUNDS, U]), ALU.subtract))
            for k in range(2):
                link(v.tensor_tensor(same[:, :, k, :], field(3), field(4 + k), ALU.is_equal))
                link(v.tensor_scalar(same[:, :, k, :], same[:, :, k, :], -1.0, BIG, ALU.add, ALU.mult))
            link(v.tensor_copy(edge_mask[:, :, :, :], same[:, :, :, :]))
            link(v.memset(edge_mask[:, :, 0, 0:1], -BIG))
            link(v.memset(edge_mask[:, :, 1, U - 1:U], -BIG))
            for k in range(2):
                tmp = [cgrid[:, q * ROUNDS * U:(q + 1) * ROUNDS * U] for q in range(2)]
                link(v.tensor_copy(tmp[0].rearrange("p (j u) -> p j u", u=U), same[:, :, k, :]))
                c = cell[:, k, :, :].rearrange("p j u -> p (j u)")
                if k == 0:
                    link(v.tensor_tensor_scan(tmp[1], c, tmp[0], 0.0, ALU.add, ALU.min))
                else:
                    link(v.tensor_tensor_scan(tmp[1][:, ::-1], c[:, ::-1], tmp[0][:, ::-1], 0.0, ALU.add, ALU.min))
                link(v.tensor_copy(reach[:, :, k, :], tmp[1].rearrange("p (j u) -> p j u", u=U)))
            link(v.tensor_copy(ends[:, :, 0], reach[:, :, 0, U - 1]))
            v.tensor_copy(ends[:, :, 1], reach[:, :, 1, 0]).then_inc(meta_ready, 1)
            dve.wait_ge(meta_ready, 1)
            dve.wait_ge(t_filled, (STEPS + 1) * NJ)

            def row_index(r, fields, types, signal):
                j = bass.ds(r.number, 1)
                f = lambda k: recs[:, j, :, k].rearrange("p j u -> p (j u)")
                v.scalar_tensor_tensor(idx[:, r.par, :], f(0), float(types), f(fields), ALU.mult, ALU.add).then_inc(signal[r.par], 1)

            def make_onehot(r, signal):
                d = dstl[:, bass.ds(r.number, 1), :].rearrange("p j u -> p (j u)").unsqueeze(2).broadcast_to([P, U, NODES])
                v.tensor_tensor(onehot[:, r.par, :, :], iota_n[:, :].unsqueeze(1).broadcast_to([P, U, NODES]), d,
                                ALU.is_equal).then_inc(signal, 1)

            def score(r, g):
                dve.wait_ge(kv_landed[r.par][g], r.loads(GU))
                for pr in range(2 * g, 2 * g + 2):
                    dve.wait_ge(qe_ready[pr], r.done)
                    k = kv[:, r.par, 2 * pr:2 * pr + 2, 0:C]
                    ins = v.tensor_tensor(k, k, b_qe[pr % 2][:, :].rearrange("p (a c) -> p a c", a=2), ALU.mult)
                    ins.then_inc(qe_used[pr], 1)
                dve.wait_ge(qe_used[2 * g], r.done)
                dve.wait_ge(qe_used[2 * g + 1], r.done)
                for u in range(g * GU, g * GU + GU, 4):
                    v.tensor_reduce(S[:, :, u:u + 4].rearrange("p h u -> p u h"),
                                    kv[:, r.par, u:u + 4, 0:C].rearrange("p u (h d) -> p u h d", h=H),
                                    AX.X, ALU.add).then_inc(scored[g], 1)

            def normalise(f):
                dve.wait_ge(agg_done, f.done)
                v.tensor_scalar_max(den[:NODES, :], b_agg[:NODES, C:C + H], 0.5).then_inc(den_ready, 1)
                dve.wait_ge(den_ready, f.done)
                v.reciprocal(rden[:NODES, :], den[:NODES, :]).then_inc(rden_ready, 1)
                dve.wait_ge(rden_ready, f.done)
                v.tensor_tensor(hN[:NODES, :].rearrange("p (h d) -> p h d", h=H),
                                b_agg[:NODES, 0:C].rearrange("p (h d) -> p h d", h=H),
                                rden[:NODES, :].unsqueeze(2).broadcast_to([NODES, H, D]), ALU.mult).then_inc(hN_ready, 1)
                dve.wait_ge(hN_ready, f.done)
                wait(dve, hT_filled[HALVES - 1], f.number)
                for t in range(NT):
                    last = v.tensor_scalar(hm[:NODES, t, :], hN[:NODES, :], calpha[:NODES, bass.ds(f.number, 1), t],
                                           None, ALU.mult)
                last.then_inc(hm_ready, 1)

            def stats(f):
                dve.wait_ge(wa_done, f.done)
                dve.wait_ge(xs_ready, f.done)
                v.tensor_tensor(z[:NODES, :], xs[:NODES, :], b_out[:NODES, 0:C], ALU.add).then_inc(z_ready, 1)
                dve.wait_ge(z_ready, f.done)
                v.bn_stats(st6[:NODES, :], z[:NODES, :]).then_inc(st_ready, 1)
                settle(dve, const_ready)
                dve.wait_ge(st_ready, f.done)
                v.bn_aggr(mv[:NODES, :], st6[:NODES, :]).then_inc(mv_ready, 1)

            def norm_rows(f):
                dve.wait_ge(sd_ready, f.done)
                v.reciprocal(rstd[:NODES, :], sd[:NODES, :]).then_inc(rstd_ready, 1)
                dve.wait_ge(rstd_ready, f.done)
                wait(dve, x1_stored, f.stores_before())
                v.tensor_scalar(x1[:NODES, f.par, :], z[:NODES, :], mv[:NODES, 0:1], rstd[:NODES, 0:1],
                                ALU.subtract, ALU.mult).then_inc(x1_ready, 1)

            def make_gates(f):
                dve.wait_ge(eg_ready, f.done)
                v.tensor_scalar_add(eg1[:NODES, :], eg[:NODES, :], 1.0).then_inc(eg1_ready, 1)
                dve.wait_ge(eg1_ready, f.done)
                wait(dve, m_evac[CHUNKS - 1], f.number)
                v.reciprocal(gate[:NODES, :], eg1[:NODES, :]).then_inc(gate_ready, 1)

            def softmax(r):
                for g in range(G):
                    dve.wait_ge(scored[g], r.done)
                dve.wait_ge(masks_ready, r.done)
                flat = lambda t: t.rearrange("p h u -> p (h u)")
                v.tensor_tensor_scan(flat(FB[:, 0, :, :]), flat(masks[:, 0, :, :]), flat(S[:, :, :]), -BIG, ALU.add, ALU.max)
                v.tensor_tensor_scan(flat(FB[:, 1, :, :])[:, ::-1], flat(masks[:, 1, :, :])[:, ::-1],
                                     flat(S[:, :, :])[:, ::-1], -BIG, ALU.add, ALU.max).then_inc(scanned, 1)

            def softmax_carry(r):
                dve.wait_ge(carry_copied, r.done)
                v.tensor_tensor_scan(carry[:, 0, 1:P + 1], carry_in[:, 1, :], carry_in[:, 0, :], -BIG, ALU.add, ALU.max)
                v.tensor_tensor_scan(carry[:, 1, 0:P][:, ::-1], carry_in[:, 3, :][:, ::-1], carry_in[:, 2, :][:, ::-1],
                                     -BIG, ALU.add, ALU.max).then_inc(carried, 1)
                dve.wait_ge(backT, r.done)
                pn = b_out[:, C + RT:C + RT + 2 * H].rearrange("p (k h) -> p k h", k=2).unsqueeze(3).broadcast_to([P, 2, H, U])
                re = reach[:, bass.ds(r.number, 1), :, :].rearrange("p j k u -> p (j k) u").unsqueeze(2).broadcast_to([P, 2, H, U])
                v.tensor_tensor(m2[:, :, :, :], pn, re, ALU.add).then_inc(m_a, 1)
                dve.wait_ge(m_a, r.done)
                v.tensor_tensor(m2[:, :, :, :], m2[:, :, :, :], FB[:, :, :, :], ALU.max).then_inc(m_b, 1)
                dve.wait_ge(m_b, r.done)
                v.tensor_tensor(mx[:, :, :], m2[:, 0, :, :], m2[:, 1, :, :], ALU.max).then_inc(m_c, 1)
                dve.wait_ge(m_c, r.done)
                v.tensor_tensor(dd[:, :, :], S[:, :, :], mx[:, :, :], ALU.subtract).then_inc(d_ready, 1)

            def weigh(r):
                dve.wait_ge(ex_ready, r.done)
                for g in range(G):
                    u = slice(g * GU, g * GU + GU)
                    w = kv[:, r.par, u, C:2 * C].rearrange("p u (h d) -> p u h d", h=H)
                    e = kv[:, r.par, u, 2 * C:ROW].unsqueeze(3).broadcast_to([P, GU, H, D])
                    v.tensor_tensor(w, w, e, ALU.mult).then_inc(weighted[g], 1)

            def l0(r):
                f = None if r.first else r.last()
                score(r, 0)
                if f:
                    normalise(f)
                    if not r.final:
                        row_index(r.next(), 1, ET, idx_ready)
                score(r, 1)
                score(r, 2)
                if f:
                    stats(f)
                score(r, 3)
                if f:
                    norm_rows(f)
                softmax(r)
                if f:
                    make_gates(f)
                softmax_carry(r)
                wait(dve, agg_done, r.number)
                if not r.final:
                    make_onehot(r.next(), oh_ready)
                weigh(r)

            row_index(Round(dve, 0, 0), 1, ET, idx_ready)
            row_index(Round(dve, 0, 1), 1, ET, idx_ready)
            make_onehot(Round(dve, 0, 0), oh_ready)
            rounds(dve, l0)
            f = Round(dve, LAST, 1)
            normalise(f)
            stats(f)
            norm_rows(f)
            make_gates(f)

            def finish(f):
                wait(dve, l_y, f.number)
                dve.wait_ge(l_agg, f.done)
                dve.wait_ge(l_x[f.par], f.loads(1))
                v.scalar_tensor_tensor(z[:NODES, :], bank[f.par][:NODES, 0:C], 0.0, xb[:NODES, f.par, :],
                                       ALU.max, ALU.add).then_inc(l_z, 1)
                dve.wait_ge(l_z, f.done)
                v.bn_stats(st6[:NODES, :], z[:NODES, :]).then_inc(l_st, 1)
                settle(dve, const_ready)
                dve.wait_ge(l_st, f.done)
                v.bn_aggr(mv[:NODES, :], st6[:NODES, :]).then_inc(l_mv, 1)
                dve.wait_ge(l_sd, f.done)
                v.reciprocal(rstd[:NODES, :], sd[:NODES, :]).then_inc(l_rstd, 1)
                dve.wait_ge(l_rstd, f.done)
                wait(dve, l_out, f.stores_before())
                v.tensor_scalar(x1[:NODES, f.par, :], z[:NODES, :], mv[:NODES, 0:1], rstd[:NODES, 0:1],
                                ALU.subtract, ALU.mult).then_inc(l_y, 1)

            def l1(r):
                wait(dve, l_agg, r.before)
                make_onehot(r, l_oh0)
                dve.wait_ge(l_oh0, r.done)
                w = norms[:, bass.ds(r.number, 1), :].rearrange("p j u -> p (j u)").unsqueeze(2).broadcast_to([P, U, NODES])
                o = onehot[:, r.par, :, :]
                v.tensor_tensor(o, o, w, ALU.mult).then_inc(l_oh, 1)
                if not r.first:
                    finish(r.last())
                    if not r.final:
                        row_index(r.next(), 2, RT, l_idx)

            row_index(Round(dve, 0, 0), 2, RT, l_idx)
            row_index(Round(dve, 0, 1), 2, RT, l_idx)
            wait(dve, x1_stored, 16 * ROUNDS)
            rounds(dve, l1)
            finish(Round(dve, LAST, 1))


def kernel(**inputs):
    import numpy as np
    import concourse.bacc as bacc
    from concourse.bass_utils import run_bass_kernel_spmd

    given = {k: np.asarray(v) for k, v in inputs.items()}
    x = np.zeros((NPAD, C), given["x"].dtype)
    x[:N] = given["x"]
    nt = np.zeros(NPAD, given["node_type_3"].dtype)
    nt[:N] = given["node_type_3"]
    dst = given["dst"]
    rec = np.zeros((EPAD, FIELDS), dst.dtype)
    for k, name in enumerate(("src", "edge_type_5", "edge_type_16")):
        rec[:E, k] = given[name]
    rec[:, 3:] = FAR
    rec[:E, 3] = dst
    rec[0, 4] = -1
    rec[1:E + 1, 4] = dst
    rec[:E - 1, 5] = dst[1:]
    norm = np.zeros(EPAD, given["edge_weight1"].dtype)
    norm[:E] = given["edge_weight1"][:, 0]
    grid = np.full(P * COUNT_COLS, FAR, dst.dtype)
    grid[:E] = dst
    arrays = {
        "x": x, "nt_rows": nt.reshape(ROUNDS, NODES).T, "rec": rec, "norm": norm,
        "dst_grid": grid.reshape(P, COUNT_COLS),
        "Wk": given["L0_gnn_Wk"], "Wq": given["L0_gnn_Wq"], "Wv": given["L0_gnn_Wv"],
        "Ratt": given["L0_gnn_Ratt"], "Rmsg": given["L0_gnn_Rmsg"], "pri": given["L0_gnn_pri"].T,
        "Wa": given["L0_gnn_Wa"], "skip": given["L0_gnn_skip"], "Wr": given["L1_gnn_weight"],
        "gate_w": given["L1_gnn_gate_weight"][:, :, 0].T,
    }
    nc = bacc.Bacc("TRN2", target_bir_lowering=False, num_devices=1)
    sent, args = {}, {}
    for name, a in arrays.items():
        sent[f"in_{name}"] = np.ascontiguousarray(a)
        args[name] = nc.dram_tensor(f"in_{name}", a.shape, mybir.dt.from_np(a.dtype), kind="ExternalInput").ap()
    out = nc.dram_tensor("out", (NPAD, C), F32, kind="ExternalOutput").ap()
    build(nc, out=out, **args)
    result = run_bass_kernel_spmd(nc, [sent], core_ids=[0])
    return result.results[0]["out"][:N]
```

```python
from contextlib import ExitStack

import concourse.bass as bass
from concourse import mybir

F32 = mybir.dt.float32
F32R = mybir.dt.float32r
I32 = mybir.dt.int32
ALU = mybir.AluOpType
ACT = mybir.ActivationFunctionType
AX = mybir.AxisListType

P = 128
C = 256
HALVES = C // P
H, D = 8, 32
NT, ET, RT = 3, 5, 16
N, E = 3125, 50000
NODES = 112
ROUNDS = -(-N // NODES)
NPAD = ROUNDS * NODES
U = 16
G, GU = 4, 4
ROUND_EDGES = P * U
EPAD = E + ROUND_EDGES
COUNT_COLS = -(-E // P)
FAR = 1 << 20
BIG = 1e30
ROW = 2 * C + H
SUPER = 4
STEPS = ROUNDS // SUPER
EPS = 1e-5
CHUNKS = RT // 2
QB = U // 2 // 2
MB = CHUNKS // 2
LAST = ROUNDS // 2 - 1
PARTS = 4
FIELDS = 6


class Round:

    def __init__(self, eng, i, par):
        self.eng, self.i, self.par = eng, i, par
        self.number = 2 * i + par
        self.done = 2 * i + (par + 1)
        self.before = 2 * i + (par - 1)
        self.first = isinstance(i, int) and self.number == 0
        self.final = isinstance(i, int) and self.number == ROUNDS - 1

    @property
    def older(self):
        return None if isinstance(self.i, int) and self.i == 0 else Round(self.eng, self.i - 1, self.par)

    def nth(self, n, k):
        return self.i * (2 * n) + (self.par * n + k)

    def loads(self, n):
        return self.i * (16 * n) + 16 * n

    def stores_before(self):
        return self.i * 32 + 16 * self.par

    def stores(self):
        return self.i * 32 + 16 * (self.par + 1)

    def last(self):
        return Round(self.eng, self.i, 0) if self.par else Round(self.eng, self.i - 1, 1)

    def next(self):
        return Round(self.eng, self.i, 1) if self.par == 0 else Round(self.eng, self.i + 1, 0)


def settle(eng, sem):
    eng.wait_ge(sem, 1)


def wait(eng, sem, value):
    if not (isinstance(value, int) and value <= 0):
        eng.wait_ge(sem, value)


def build(nc, x, nt_rows, rec, norm, dst_grid, Wk, Wq, Wv, Ratt, Rmsg, pri, Wa, skip, Wr, gate_w, out):
    ktab = nc.dram_tensor("kv_table", [NPAD * ET, 2 * C], F32).ap()
    qtab = nc.dram_tensor("query_table", [NPAD, 2 * C], F32).ap()
    x1tab = nc.dram_tensor("x1_table", [NPAD, C], F32).ap()
    mtab = nc.dram_tensor("message_table", [NPAD * RT, C], F32).ap()
    ktab_n = ktab.rearrange("(n r) c -> n (r c)", r=ET)
    mtab_n = mtab.rearrange("(n r) c -> n (r c)", r=RT)

    ctx = ExitStack()
    with ctx:
        def sb(name, shape, dt=F32, life=ctx):
            return life.enter_context(nc.sbuf_tensor(name, shape, dt))

        def sem(name):
            return ctx.enter_context(nc.semaphore(name))

        def sems(name, n):
            return [sem(f"{name}{k}") for k in range(n)]

        norms = sb("norms", [P, ROUNDS, U])
        dstl = sb("dstl", [P, ROUNDS, U])
        edge_mask = sb("edge_mask", [P, ROUNDS, 2, U])
        reach = sb("reach", [P, ROUNDS, 2, U])
        ends = sb("ends", [P, ROUNDS, 2])
        rows = sb("rows", [P, 2, ROUNDS, U], I32)
        starts = sb("starts", [1, ROUNDS], I32)
        ones = sb("ones", [P, 1])
        ident = sb("ident", [P, P])
        ident_r = sb("ident_r", [P, P], F32R)
        iota_n = sb("iota_n", [P, NODES])
        base = sb("base", [P, ROUNDS])
        nmask = sb("nmask", [P, ROUNDS + SUPER, NT])
        calpha = sb("calpha", [P, ROUNDS, NT])
        keep = sb("keep", [P, ROUNDS])
        alpha = sb("alpha", [P, NT])
        gw = sb("gw", [P, HALVES, RT])
        gw_r = sb("gw_r", [P, 2, HALVES, RT], F32R)
        eps = sb("eps", [P, 1])
        idx = sb("idx", [P, 2, U], I32)
        st6 = sb("st6", [P, 6])
        mv = sb("mv", [P, 2])
        sd = sb("sd", [P, 1])
        rstd = sb("rstd", [P, 1])
        den = sb("den", [P, H])
        rden = sb("rden", [P, H])
        gsum = sb("gsum", [P, 2, H])
        eg = sb("eg", [P, RT])
        eg1 = sb("eg1", [P, RT])
        gate = sb("gate", [P, 2, RT])

        SN = SUPER * NODES
        with ExitStack() as t_life:
            def tsb(name, shape, dt=F32):
                return sb(name, shape, dt, t_life)
            x_all = tsb("x_all", [NODES, ROUNDS + SUPER, C])
            w_r = tsb("w_r", [P, 2, 3, NT, HALVES, C], F32R)
            rel_r = tsb("rel_r", [P, 2, 2, HALVES, ET, P], F32R)
            xm = tsb("xm", [NODES, NT, SUPER, C])
            kvT_r = tsb("kvT_r", [P, 2, 2, HALVES, SN], F32R)
            tstage = tsb("tstage", [NODES, 2, ET, 2 * C])
            qstage_r = tsb("qstage_r", [NODES, SUPER, 2, C], F32R)
            recs = tsb("recs", [P, ROUNDS, U, FIELDS], I32)
            cell = tsb("cell", [P, 2, ROUNDS, U])
            with ExitStack() as first_life:
                w_in = sb("w_in", [P, 3, NT, HALVES, C], F32, first_life)
                rel = sb("rel", [P, 2, HALVES, ET, P], F32, first_life)
                pris = sb("pris", [P, HALVES, ET], F32, first_life)
                nt_i = sb("nt_i", [P, ROUNDS], I32, first_life)
                skips = sb("skips", [P, NT], F32, first_life)
                grid_i = sb("grid_i", [P, COUNT_COLS], I32, first_life)
                grid_f = sb("grid_f", [P, COUNT_COLS], F32, first_life)
                grid_o = sb("grid_o", [P, COUNT_COLS], F32, first_life)
                cnt = sb("cnt", [P, ROUNDS], F32, first_life)
            xmT_r = tsb("xmT_r", [P, 2, NT, HALVES, SN], F32R)
            same = tsb("same", [P, ROUNDS, 2, U])
            line = tsb("line", [P, 2, ROUNDS * U])
        with ExitStack() as l_life:
            def lsb(name, shape, dt=F32):
                return sb(name, shape, dt, l_life)
            xb = lsb("xb", [NODES, 2, C])
            x1 = lsb("x1", [NODES, 2, C])
            z = lsb("z", [NODES, C])
            kv = lsb("kv", [P, 2, U, ROW])
            with ExitStack() as m_life:
                def msb(name, shape, dt=F32):
                    return sb(name, shape, dt, m_life)
                wr_r = msb("wr_r", [P, 2, HALVES, RT, C], F32R)
                mstage = msb("mstage", [NODES, 2, RT // PARTS, C])
                wa = msb("wa", [P, NT, HALVES, C])
                onehot_r = msb("onehot_r", [P, 2, U, NODES], F32R)
                onehotT_r = msb("onehotT_r", [NODES, U, P], F32R)
                qb_r = msb("qb_r", [NODES, 2, 2, C], F32R)
                S = msb("S", [P, H, U])
                masks = msb("masks", [P, 2, H, U])
                m2 = masks
                FB = msb("FB", [P, 2, H, U])
                carry_in = msb("carry_in", [H, 4, P])
                carry = msb("carry", [H, 2, P + 1])
                hN = msb("hN", [NODES, C])
                hm = msb("hm", [NODES, NT, C])
                hmT = msb("hmT", [P, HALVES, NT, NODES])
                x1T_r = msb("x1T_r", [P, 2, 2, HALVES, NODES], F32R)
            onehot_w = lsb("onehot_w", [P, 2, U, NODES])
        wr = kv[:, 1, :, :].rearrange("p u c -> p (u c)")[:, 0:HALVES * RT * C].rearrange(
            "p (h r c) -> p h r c", h=HALVES, r=RT)

        bank = [ctx.enter_context(nc.psum_tensor(f"bank{k}", [P, 512], F32)) for k in range(8)]
        b_x1T = bank[5][:, C + RT:C + RT + HALVES * NODES]
        b_qe, b_ohT, b_agg, b_tmp, b_out, b_m = bank[0:2], bank[2], bank[3], bank[4], bank[5], bank[6:8]

        ld_grid, ld_x, ld_wa, ld_wr, ld_gw, ld_rel, ld_small, ld_rec = (sem(n) for n in (
            "ld_grid", "ld_x", "ld_wa", "ld_wr", "ld_gw", "ld_rel", "ld_small", "ld_rec"))
        ld_w, w_high, w_low = sems("ld_w", 3), sem("w_high"), sem("w_low")
        rel_high, rel_low, wr_high, wr_low, gw_high, gw_low = (sem(n) for n in (
            "rel_high", "rel_low", "wr_high", "wr_low", "gw_high", "gw_low"))
        const_ready, zeroed, rel_ready, ident_high = (sem(n) for n in (
            "const_ready", "zeroed", "rel_ready", "ident_high"))
        pool_step = sem("pool_step")
        counted = sem("counted")
        alpha_exp, grid_ready, meta_step = sem("alpha_exp"), sem("grid_ready"), sem("meta_step")
        cnt_summed, starts_ready, tables_over, mask_ready = (sem(n) for n in (
            "cnt_summed", "starts_ready", "tables_over", "mask_ready"))
        xm_ready, x_filled, x_high, x_low, t_filled, t_act, t_dve = (sem(n) for n in (
            "xm_ready", "x_filled", "x_high", "x_low", "t_filled", "t_act", "t_dve"))
        t_stored, q_stored = sems("t_stored", 2), sems("q_stored", 2)

        q_loaded, x_loaded = sems("q_loaded", 2), sems("x_loaded", 2)
        idx_ready, oh_ready = sems("idx_ready", 2), sem("oh_ready")
        kv_landed = [sems(f"kv_landed{p}_", G) for p in range(2)]
        ohT_filled, ohT_ready = sems("ohT_filled", G), sems("ohT_ready", G)
        qe_ready, qe_used = sems("qe_ready", 2), sems("qe_used", 2)
        scored, carry_ends = sems("scored", G), sem("carry_ends")
        masks_ready, scanned, carryT, carry_copied = (sem(n) for n in (
            "masks_ready", "scanned", "carryT", "carry_copied"))
        carried, backT, m_a, m_b, m_c, d_ready, ex_ready = (sem(n) for n in (
            "carried", "backT", "m_a", "m_b", "m_c", "d_ready", "ex_ready"))
        weighted = sems("weighted", G)
        agg_done = sem("agg_done")
        den_ready, rden_ready, hN_ready, hm_ready = (sem(n) for n in (
            "den_ready", "rden_ready", "hN_ready", "hm_ready"))
        hT_filled, hT_ready = sems("hT_filled", HALVES), sems("hT_ready", HALVES)
        wa_done, xs_ready, z_ready, st_ready, mv_ready, sd_ready, rstd_ready, x1_ready = (sem(n) for n in (
            "wa_done", "xs_ready", "z_ready", "st_ready", "mv_ready", "sd_ready", "rstd_ready", "x1_ready"))
        x1T_filled, x1T_high, x1T_low, gate_psum, eg_ready, eg1_ready, gate_ready = (sem(n) for n in (
            "x1T_filled", "x1T_high", "x1T_low", "gate_psum", "eg_ready", "eg1_ready", "gate_ready"))
        m_filled, m_evac = sems("m_filled", 2), sems("m_evac", 2)
        m_stored = sems("m_stored", PARTS)
        x1_stored = sem("x1_stored")

        l_idx, l_oh0, l_oh, l_agg = sems("l_idx", 2), sem("l_oh0"), sem("l_oh"), sem("l_agg")
        l_landed = [sems(f"l_landed{p}_", 2) for p in range(2)]
        l_x = sems("l_x", 2)
        l_z, l_st, l_mv, l_sd, l_rstd, l_y = (sem(n) for n in (
            "l_z", "l_st", "l_mv", "l_sd", "l_rstd", "l_y"))
        l_out = sem("l_out")

        block = ctx.enter_context(nc.Block())

        PASSES = ((0, 0), (0, 1), (1, 0))

        JOBS = ([("kvT", k, h) for k in range(2) for h in range(HALVES)]
                + [("q", s) for s in range(SUPER)]
                + [("tab", s, q) for s in range(SUPER) for q in range(5)])
        NJ, JB = len(JOBS), 6
        TURNS = [(t, h) for t in range(NT) for h in range(HALVES)]
        NX = len(TURNS)
        TURN_AT = {NJ - 18 + 3 * n: n for n in range(NX)}

        def on_act(k):
            return JOBS[k][0] != "tab" or (JOBS[k][1] + JOBS[k][2]) % 2 == 0

        def on_dve(k):
            return JOBS[k][0] != "tab" or not on_act(k)
        A_IDX = {k: n + 1 for n, k in enumerate(k for k in range(NJ) if on_act(k))}
        D_IDX = {k: n + 1 for n, k in enumerate(k for k in range(NJ) if on_dve(k))}
        NA, ND = len(A_IDX), len(D_IDX)

        def rounds(eng, body):
            for par in range(2):
                body(Round(eng, 0, par))
            with eng.Fori(1, LAST) as i:
                for par in range(2):
                    body(Round(eng, i, par))
            for par in range(2):
                body(Round(eng, LAST, par))

        def table_part(eng, s, job, b):
            _, t, q = job
            st = tstage[:NODES, t % 2, :, :]
            eng.wait_ge(t_stored[t % 2], s * 32 + 16 * (t // 2))
            if q < 4:
                return st[:, 0:4, q * P:(q + 1) * P], b[:NODES, :].rearrange("p (r n) -> p r n", r=4)
            return st[:, 4, :], b[:NODES, :]

        @block.sync
        def _(sp):
            for k in range(2):
                sp.sem_inc(t_stored[k], 32)
                sp.sem_inc(q_stored[k], 32)
            sp.dma_start(grid_i[:, :], dst_grid).then_inc(ld_grid, 16)
            sp.dma_start(x_all[:, 0:ROUNDS, :], x.rearrange("(j p) c -> p j c", p=NODES)).then_inc(ld_x, 16)
            for k, w in enumerate((Wk, Wv, Wq)):
                sp.dma_start(w_in[:, k, :, :, :], w.rearrange("t (h p) n -> p t h n", p=P)).then_inc(ld_w[k], 16)
            sp.wait_ge(zeroed, 1)
            for k, r in enumerate((Ratt, Rmsg)):
                for h in range(H):
                    q = D * (h % 4)
                    sp.dma_start(rel[q:q + D, k, h // 4, :, q:q + D],
                                 r[:, h].rearrange("r d f -> d r f")).then_inc(ld_rel, 16)
            for h in range(H):
                q = D * (h % 4)
                sp.dma_start(pris[q:q + D, h // 4, :], pri[h:h + 1, :].to_broadcast([D, ET])).then_inc(ld_rel, 16)
            sp.wait_ge(starts_ready, 1)
            with sp.Fori(0, ROUNDS) as j:
                s = sp.value_load(starts[0:1, bass.ds(j, 1)], min_val=0, max_val=E)
                sp.dma_start(recs[:, bass.ds(j, 1), :, :].rearrange("p j u f -> p (j u f)"),
                             rec[bass.ds(s, ROUND_EDGES), :].rearrange("(p u) f -> p (u f)", p=P)).then_inc(ld_rec, 16)
                sp.dma_start(norms[:, bass.ds(j, 1), :].rearrange("p j u -> p (j u)"),
                             norm[bass.ds(s, ROUND_EDGES)].rearrange("(p u) -> p u", p=P)).then_inc(ld_rec, 16)
            with sp.Fori(1, STEPS + 1) as s:
                for t in range(SUPER):
                    ks = [JOBS.index(("tab", t, q)) for q in range(5)]
                    sp.wait_ge(t_act, s * NA + max(A_IDX[k] for k in ks if k in A_IDX))
                    sp.dma_start(qtab[bass.ds(s * SN + (t - SUPER) * NODES, NODES), :],
                                 qstage_r[:, t, :, :].rearrange("p k c -> p (k c)").bitcast(F32)).then_inc(q_stored[t % 2], 16)
                    sp.wait_ge(t_dve, s * ND + max(D_IDX[k] for k in ks if k in D_IDX))
                    sp.dma_start(ktab_n[bass.ds(s * SN + (t - SUPER) * NODES, NODES), :],
                                 tstage[:, t % 2, :, :].rearrange("p r c -> p (r c)")).then_inc(t_stored[t % 2], 16)
            sp.wait_ge(tables_over, 1)
            for h in range(HALVES):
                sp.dma_start(wr[:, h, :, :], Wr[:, h * P:(h + 1) * P, :].rearrange("r p n -> p r n")).then_inc(ld_wr, 16)
            sp.dma_start(wa[:, :, :, :], Wa.rearrange("t (h p) n -> p t h n", p=P)).then_inc(ld_wa, 16)

            def load(r):
                wait(sp, qe_used[1], r.nth(QB, -QB))
                sp.dma_start(qb_r[:, r.par, :, :].rearrange("p k c -> p (k c)").bitcast(F32),
                             qtab[bass.ds(r.number * NODES, NODES), :]).then_inc(q_loaded[r.par], 16)
                wait(sp, xs_ready, r.before)
                sp.dma_start(xb[:NODES, r.par, :], x[bass.ds(r.number * NODES, NODES), :]).then_inc(x_loaded[r.par], 16)

            def store_x1(f):
                sp.wait_ge(x1_ready, f.done)
                sp.dma_start(x1tab[bass.ds(f.number * NODES, NODES), :], x1[:NODES, f.par, :]).then_inc(x1_stored, 16)

            def store_messages(f):
                for b in range(PARTS):
                    sp.wait_ge(m_evac[1], f.nth(MB, b + 1 + MB))
                    w = RT // PARTS * C
                    sp.dma_start(mtab_n[bass.ds(f.number * NODES, NODES), b * w:(b + 1) * w],
                                 mstage[:, b % 2, :, :].rearrange("p r c -> p (r c)")).then_inc(m_stored[b], 16)

            def l0(r):
                if not r.final:
                    load(r.next())
                if r.older:
                    store_messages(r.older)
                if not r.first:
                    store_x1(r.last())
            load(Round(sp, 0, 0))
            rounds(sp, l0)
            store_messages(Round(sp, LAST, 0))
            store_x1(Round(sp, LAST, 1))
            store_messages(Round(sp, LAST, 1))
            sp.wait_ge(x1_stored, 16 * ROUNDS)

            def l1(r):
                wait(sp, l_z, r.before)
                sp.dma_start(xb[:NODES, r.par, :], x1tab[bass.ds(r.number * NODES, NODES), :]).then_inc(l_x[r.par], 16)
                if not r.first:
                    last(r.last())

            def last(f):
                sp.wait_ge(l_y, f.done)
                sp.dma_start(out[bass.ds(f.number * NODES, NODES), :], x1[:NODES, f.par, :]).then_inc(l_out, 16)
            rounds(sp, l1)
            last(Round(sp, LAST, 1))
            sp.wait_ge(l_out, 16 * ROUNDS)

        @block.gpsimd
        def _(pool):
            pool.memset(rel[:, :, :, :, :], 0.0).then_inc(zeroed, 1)
            pool.memset(x_all[:, ROUNDS:, :], 0.0)
            pool.memset(nmask[:, ROUNDS:, :], 0.0)
            pool.memset(ident[:, :], 0.0).then_inc(pool_step, 1)
            pool.memset(ones[:, :], 1.0)
            pool.memset(eps[:, :], EPS)
            pool.memset(cell[:, :, :, :], 0.0).then_inc(pool_step, 1)
            pool.iota(iota_n[:, :], pattern=[[1, NODES]], base=0, channel_multiplier=0,
                      allow_small_or_imprecise_dtypes=True)
            pool.iota(base[:, :], pattern=[[NODES, ROUNDS]], base=0, channel_multiplier=0,
                      allow_small_or_imprecise_dtypes=True)
            pool.wait_ge(pool_step, 2)
            pool.memset(cell[:, 0, :, 0:1], 2 * BIG)
            pool.memset(cell[:, 1, :, U - 1:U], 2 * BIG)
            pool.affine_select(out=ident[:, :], in_=ident[:, :], compare_op=ALU.not_equal, fill=1.0,
                               base=0, pattern=[[-1, P]], channel_multiplier=1).then_inc(const_ready, 1)
            pool.dma_start(nt_i[:NODES, :], nt_rows).then_inc(ld_small, 16)
            pool.dma_start(skips[:, :], skip.rearrange("(a t) -> a t", a=1).to_broadcast([P, NT])).then_inc(ld_small, 16)
            pool.dma_start(gw[:, :, :], gate_w.rearrange("(h p) r -> p h r", p=P)).then_inc(ld_gw, 16)

            pool.wait_ge(tables_over, 1)
            pool.memset(carry[:, 0, 0:1], -BIG)
            pool.memset(carry[:, 1, P:P + 1], -BIG).then_inc(carry_ends, 1)

            def gather(pair, table, width, indices, landed):
                for par in range(2):
                    settle(pool, const_ready)
                    if isinstance(pair, int) and par == 1 and table is ktab:
                        pool.wait_ge(wr_low, HALVES)
                    pool.wait_ge(indices[par], pair)
                    for u in range(U):
                        pool.indirect_dma_start(kv[:, par, u, 0:width], None, table,
                                                bass.IndirectOffsetOnAxis(ap=idx[:, par, u:u + 1], axis=0)
                                                ).then_inc(landed[par][u * len(landed[par]) // U], 16)

            gather(1, ktab, 2 * C, idx_ready, kv_landed)
            with pool.Fori(2, ROUNDS // 2 + 1) as pair:
                gather(pair, ktab, 2 * C, idx_ready, kv_landed)
            for b in range(PARTS):
                pool.wait_ge(m_stored[b], 16 * (ROUNDS + 1))
            pool.wait_ge(agg_done, ROUNDS)

            with pool.Fori(1, ROUNDS // 2 + 1) as pair:
                gather(pair, mtab, C, l_idx, l_landed)

        @block.tensor
        def _(pe):
            mm = nc.tensor.matmul
            pe.sem_inc(t_filled, NJ)
            pe.wait_ge(const_ready, 1)
            pe.wait_ge(counted, ROUNDS)
            mm(bank[0][0:1, 0:ROUNDS], ones[:, :], cnt[:, :], start=True, stop=True).then_inc(cnt_summed, 1)
            pe.wait_ge(starts_ready, 1)

            def turn_x(s, n):
                t, h = TURNS[n]
                b = bank[6 + n % 2]
                if n == 0:
                    pe.wait_ge(xm_ready, s)
                wait(pe, x_low, (s - 1) * NX + (n - 1))
                for q in range(SUPER):
                    last = nc.tensor.transpose(b[:, q * NODES:(q + 1) * NODES],
                                               xm[:, t, q, h * P:(h + 1) * P], ident[:NODES, :NODES])
                last.then_inc(x_filled, 1)

            for n in range(NX):
                turn_x(1, n)
            pe.wait_ge(w_high, 3)
            pe.wait_ge(w_low, 3)
            pe.wait_ge(rel_high, 1)
            pe.wait_ge(rel_low, 1)
            with pe.Fori(1, STEPS + 1) as s:
                pe.wait_ge(x_high, s * NX)
                pe.wait_ge(x_low, s * NX)
                for k, job in enumerate(JOBS):
                    if k in TURN_AT:
                        turn_x(s + 1, TURN_AT[k])
                    b = bank[k % JB]
                    before, there = (s, k - JB) if k >= JB else (s - 1, max(j for j in range(NJ) if j % JB == k))
                    if on_dve(there):
                        pe.wait_ge(t_dve, before * ND + D_IDX[there])
                    else:
                        pe.wait_ge(t_act, before * NA + A_IDX[there])
                    if job[0] == "kvT":
                        _, kk, ho = job
                        terms = [(w_r[:, a, kk, t, h, ho * P:(ho + 1) * P], xmT_r[:, c, t, h, :])
                                 for t in range(NT) for h in range(HALVES) for a, c in PASSES]
                        for n, (lhsT, rhs) in enumerate(terms):
                            last = mm(b[:, 0:SN], lhsT, rhs, start=(n == 0), stop=(n == len(terms) - 1))
                    elif job[0] == "q":
                        o = slice(job[1] * NODES, (job[1] + 1) * NODES)
                        terms = [(xmT_r[:, a, t, h, o], w_r[:, c, 2, t, h, :])
                                 for t in range(NT) for h in range(HALVES) for a, c in PASSES]
                        for n, (lhsT, rhs) in enumerate(terms):
                            last = mm(b[:NODES, 0:C], lhsT, rhs, start=(n == 0), stop=(n == len(terms) - 1))
                    else:
                        _, t, q = job
                        o = slice(t * NODES, (t + 1) * NODES)
                        if (t, q) == (0, 0):
                            last_kv = JOBS.index(("kvT", 1, HALVES - 1))
                            pe.wait_ge(t_act, s * NA + A_IDX[last_kv])
                            pe.wait_ge(t_dve, s * ND + D_IDX[last_kv])
                        if q < 4:
                            kk, h = q // 2, q % 2
                            for n, (a, c) in enumerate(PASSES):
                                last = mm(b[:NODES, 0:4 * P], kvT_r[:, a, kk, h, o], rel_r[:, c, kk, h, 0:4, :],
                                          start=(n == 0), stop=(n == 2))
                        else:
                            for kk in range(2):
                                for h in range(2):
                                    z0 = (2 * kk + h) * P
                                    for n, (a, c) in enumerate(PASSES):
                                        last = mm(b[:NODES, z0:z0 + P], kvT_r[:, a, kk, h, o], rel_r[:, c, kk, h, 4, :],
                                                  start=(n == 0), stop=(n == 2))
                    last.then_inc(t_filled, 1)
            pe.wait_ge(tables_over, 1)
            pe.wait_ge(ld_wa, 16)
            pe.wait_ge(gw_high, 1)
            pe.wait_ge(gw_low, 1)

            def turn_onehot(r, g):
                if g == 0:
                    pe.wait_ge(oh_ready, r.done)
                if g:
                    pe.wait_ge(ohT_ready[g - 1], r.done)
                else:
                    wait(pe, ohT_ready[G - 1], r.number)
                for q in range(GU):
                    last = mm(b_ohT[:NODES, q * P:(q + 1) * P], onehot_r[:, r.par, g * GU + q, :], ident_r[:, :],
                              start=True, stop=True)
                last.then_inc(ohT_filled[g], 1)

            def hand_queries(r, g):
                if g == 0:
                    pe.wait_ge(q_loaded[r.par], r.loads(1))
                pe.wait_ge(ohT_ready[g], r.done)
                for pr in range(2 * g, 2 * g + 2):
                    wait(pe, qe_used[pr % 2], r.nth(QB, pr // 2))
                    for q in range(2):
                        for part in range(2):
                            last = mm(b_qe[pr % 2][:, q * C:(q + 1) * C], onehotT_r[:, 2 * pr + q, :],
                                      qb_r[:, r.par, part, :], start=(part == 0), stop=(part == 1))
                    last.then_inc(qe_ready[pr % 2], 1)

            def turn_h(f, h):
                if h == 0:
                    pe.wait_ge(hm_ready, f.done)
                else:
                    pe.wait_ge(hT_ready[h - 1], f.done)
                for t in range(NT):
                    last = nc.tensor.transpose(b_tmp[:, t * NODES:(t + 1) * NODES],
                                               hm[:NODES, t, h * P:(h + 1) * P], ident[:NODES, :NODES])
                last.then_inc(hT_filled[h], 1)

            def project(f):
                for h in range(HALVES):
                    pe.wait_ge(hT_ready[h], f.done)
                for n, (h, t) in enumerate((h, t) for h in range(HALVES) for t in range(NT)):
                    last = mm(b_out[:NODES, 0:C], hmT[:, h, t, :], wa[:, t, h, :],
                              start=(n == 0), stop=(n == 2 * NT - 1))
                last.then_inc(wa_done, 1)

            def turn_x1(f):
                pe.wait_ge(x1_ready, f.done)
                for h in range(HALVES):
                    last = nc.tensor.transpose(b_x1T[:, h * NODES:(h + 1) * NODES],
                                               x1[:NODES, f.par, h * P:(h + 1) * P], ident[:NODES, :NODES])
                last.then_inc(x1T_filled, 1)

            def gates(f):
                pe.wait_ge(x1T_high, f.done)
                pe.wait_ge(x1T_low, f.done)
                terms = [(h, a, c) for h in range(HALVES) for a, c in PASSES]
                for n, (h, a, c) in enumerate(terms):
                    last = mm(b_out[:NODES, C:C + RT], x1T_r[:, f.par, a, h, :], gw_r[:, c, h, :],
                              start=(n == 0), stop=(n == len(terms) - 1))
                last.then_inc(gate_psum, 1)

            def message(f, c):
                pe.wait_ge(m_evac[c % 2], f.nth(MB, c // 2 + MB))
                terms = [(h, a, w) for h in range(HALVES) for a, w in PASSES]
                for n, (h, a, w) in enumerate(terms):
                    last = mm(b_m[c % 2][:NODES, :], x1T_r[:, f.par, a, h, :], wr_r[:, w, h, 2 * c:2 * c + 2, :],
                              start=(n == 0), stop=(n == len(terms) - 1))
                last.then_inc(m_filled[c % 2], 1)

            def turn_carry(r):
                pe.wait_ge(scanned, r.done)
                pe.wait_ge(masks_ready, r.done)
                for k, a in enumerate((FB[:, 0, :, U - 1], gsum[:, 0, :], FB[:, 1, :, 0], gsum[:, 1, :])):
                    last = nc.tensor.transpose(b_tmp[:H, k * P:(k + 1) * P], a, ident[:, :])
                last.then_inc(carryT, 1)

            def turn_back(r):
                settle(pe, const_ready)
                pe.wait_ge(carried, r.done)
                nc.tensor.transpose(b_tmp[:, 0:H], carry[:, 0, 0:P], ident[:H, :H])
                nc.tensor.transpose(b_tmp[:, H:2 * H], carry[:, 1, 1:P + 1],
                                    ident[:H, :H]).then_inc(backT, 1)

            def aggregate(r, g):
                pe.wait_ge(weighted[g], r.done)
                if g == 0:
                    wait(pe, hN_ready, r.number)
                for u in range(g * GU, g * GU + GU):
                    last = mm(b_agg[:NODES, 0:C + H], onehot_r[:, r.par, u, :].bitcast(F32), kv[:, r.par, u, C:ROW],
                              start=(u == 0), stop=(u == U - 1))
                if g == G - 1:
                    last.then_inc(agg_done, 1)

            def l0(r):
                f = None if r.first else r.last()

                def messages(*chunks):
                    if r.older:
                        for c in chunks:
                            message(r.older, c)
                n = None if r.final else r.next()
                if f:
                    turn_h(f, 0)
                messages(0)
                hand_queries(r, 3)
                if f:
                    turn_h(f, 1)
                    project(f)
                turn_carry(r)
                messages(1, 2)
                turn_back(r)
                if n:
                    turn_onehot(n, 0)
                messages(3)
                if n:
                    turn_onehot(n, 1)
                messages(4)
                if n:
                    hand_queries(n, 0)
                if f:
                    turn_x1(f)
                messages(5)
                aggregate(r, 0)
                aggregate(r, 1)
                if n:
                    turn_onehot(n, 2)
                    hand_queries(n, 1)
                aggregate(r, 2)
                if n:
                    turn_onehot(n, 3)
                if f:
                    gates(f)
                aggregate(r, 3)
                if n:
                    hand_queries(n, 2)
                messages(6, 7)

            first = Round(pe, 0, 0)
            for g in range(G):
                turn_onehot(first, g)
            for g in range(G - 1):
                hand_queries(first, g)
            pe.wait_ge(wr_high, HALVES)
            pe.wait_ge(wr_low, HALVES)
            rounds(pe, l0)
            f = Round(pe, LAST, 1)
            for h in range(HALVES):
                turn_h(f, h)
            project(f)
            for c in range(CHUNKS):
                message(Round(pe, LAST, 0), c)
            turn_x1(f)
            gates(f)
            for c in range(CHUNKS):
                message(f, c)

            def l1(r):
                wait(pe, l_z, r.before)
                pe.wait_ge(l_oh, r.done)
                for u in range(U):
                    if u % (U // 2) == 0:
                        pe.wait_ge(l_landed[r.par][u * 2 // U], r.loads(U // 2))
                    last = mm(bank[r.par][:NODES, 0:C], onehot_w[:, r.par, u, :], kv[:, r.par, u, 0:C],
                              start=(u == 0), stop=(u == U - 1))
                last.then_inc(l_agg, 1)
            pe.wait_ge(qe_used[1], ROUNDS * QB)
            rounds(pe, l1)

        @block.scalar
        def _(act):
            a = nc.scalar.activation
            act.sem_inc(t_act, NA)
            for k in range(2):
                act.sem_inc(m_evac[k], MB)
            for b in range(PARTS):
                act.sem_inc(m_stored[b], 16)
            act.wait_ge(ld_small, 32)
            a(alpha[:, :], skips[:, :], ACT.Exp, scale=-1.0).then_inc(alpha_exp, 1)
            for k in range(3):
                act.wait_ge(ld_w[k], 16)
                a(w_r[:, 0, k, :, :, :], w_in[:, k, :, :, :], ACT.Copy).then_inc(w_high, 1)
            act.wait_ge(const_ready, 1)
            a(ident_r[:, :], ident[:, :], ACT.Copy).then_inc(ident_high, 1)
            act.wait_ge(ld_gw, 16)
            a(gw_r[:, 0, :, :], gw[:, :, :], ACT.Copy).then_inc(gw_high, 1)
            act.wait_ge(rel_ready, HALVES)
            a(rel_r[:, 0, :, :, :, :], rel[:, :, :, :, :], ACT.Copy).then_inc(rel_high, 1)

            def keep_xT(s, n):
                t, h = TURNS[n]
                act.wait_ge(x_filled, (s - 1) * NX + (n + 1))
                a(xmT_r[:, 0, t, h, :], bank[6 + n % 2][:, 0:SN], ACT.Copy).then_inc(x_high, 1)

            act.wait_ge(w_low, 3)
            act.wait_ge(rel_low, 1)
            act.wait_ge(starts_ready, 1)
            act.wait_ge(mask_ready, 1)
            for n in range(NX):
                keep_xT(1, n)
            with act.Fori(1, STEPS + 1) as s:
                for k, job in enumerate(JOBS):
                    if k in TURN_AT:
                        keep_xT(s + 1, TURN_AT[k])
                    if not on_act(k):
                        continue
                    act.wait_ge(t_filled, s * NJ + (k + 1))
                    b = bank[k % JB]
                    if job[0] == "kvT":
                        o, i = kvT_r[:, 0, job[1], job[2], :], b[:, 0:SN]
                    elif job[0] == "q":
                        t = job[1]
                        act.wait_ge(q_stored[t % 2], s * 32)
                        o, i = qstage_r[:, t, 0, :], b[:NODES, 0:C]
                    else:
                        o, i = table_part(act, s, job, b)
                    a(o, i, ACT.Copy).then_inc(t_act, 1)
            act.wait_ge(tables_over, 1)

            def spread_masks(r):
                wait(act, d_ready, r.number)
                j = bass.ds(r.number, 1)
                a(masks[:, :, :, :], edge_mask[:, j, :, :].rearrange("p j k u -> p (j k) u").unsqueeze(2)
                  .broadcast_to([P, 2, H, U]), ACT.Copy)
                a(gsum[:, :, :], ends[:, j, :].rearrange("p j k -> p (j k)").unsqueeze(2)
                  .broadcast_to([P, 2, H]), ACT.Copy).then_inc(masks_ready, 1)

            def keep_onehotT(r, g):
                act.wait_ge(ohT_filled[g], r.done)
                a(onehotT_r[:, g * GU:(g + 1) * GU, :], b_ohT[:NODES, :].rearrange("p (a b) -> p a b", a=GU),
                  ACT.Copy).then_inc(ohT_ready[g], 1)

            def keep_hT(f, h):
                act.wait_ge(hT_filled[h], f.done)
                a(hmT[:, h, :, :], b_tmp[:, 0:NT * NODES].rearrange("p (t n) -> p t n", t=NT),
                  ACT.Copy).then_inc(hT_ready[h], 1)

            def residual(f):
                act.wait_ge(x_loaded[f.par], f.loads(1))
                wait(act, x1_ready, f.number)
                a(z[:, :], xb[:NODES, f.par, :], ACT.Copy,
                  scale=keep[:NODES, bass.ds(f.number, 1)]).then_inc(xs_ready, 1)

            def deviation(f):
                act.wait_ge(mv_ready, f.done)
                a(sd[:NODES, :], mv[:NODES, 1:2], ACT.Sqrt, bias=eps[:NODES, :]).then_inc(sd_ready, 1)

            def keep_x1T(f):
                act.wait_ge(x1T_filled, f.done)
                a(x1T_r[:, f.par, 0, :, :], b_x1T.rearrange("p (h n) -> p h n", h=HALVES),
                  ACT.Copy).then_inc(x1T_high, 1)

            def gate_exps(f):
                act.wait_ge(gate_psum, f.done)
                a(eg[:NODES, :], b_out[:NODES, C:C + RT], ACT.Exp, scale=-1.0).then_inc(eg_ready, 1)

            def keep_message(f, c):
                b = c * PARTS // CHUNKS
                if c == 0:
                    act.wait_ge(gate_ready, f.done)
                if c % (CHUNKS // PARTS) == 0:
                    if b < 2:
                        act.wait_ge(m_stored[b + 2], f.stores_before() + 16)
                    else:
                        act.wait_ge(m_stored[b - 2], f.stores() + 16)
                act.wait_ge(m_filled[c % 2], f.nth(MB, c // 2 + 1))
                for k in range(2):
                    q = 2 * c + k
                    last = a(mstage[:, b % 2, q % (RT // PARTS), :], b_m[c % 2][:NODES, k * C:(k + 1) * C],
                             ACT.Copy, scale=gate[:NODES, f.par, q:q + 1])
                last.then_inc(m_evac[c % 2], 1)

            def keep_carry(r):
                act.wait_ge(carryT, r.done)
                a(carry_in[:, :, :], b_tmp[:H, :].rearrange("p (k n) -> p k n", k=4), ACT.Copy).then_inc(carry_copied, 1)

            def exps(r):
                act.wait_ge(d_ready, r.done)
                a(kv[:, r.par, :, 2 * C:ROW], S[:, :, :].rearrange("p h u -> p u h"), ACT.Exp).then_inc(ex_ready, 1)

            act.wait_ge(mask_ready, 1)

            def l0(r):
                f = None if r.first else r.last()

                def messages(*chunks):
                    if r.older:
                        for c in chunks:
                            keep_message(r.older, c)
                n = None if r.final else r.next()
                spread_masks(r)
                if f:
                    keep_hT(f, 0)
                messages(0)
                if f:
                    keep_hT(f, 1)
                    residual(f)
                keep_carry(r)
                messages(1)
                if f:
                    deviation(f)
                messages(2)
                if n:
                    keep_onehotT(n, 0)
                messages(3)
                if n:
                    keep_onehotT(n, 1)
                exps(r)
                messages(4)
                if f:
                    keep_x1T(f)
                messages(5)
                if n:
                    keep_onehotT(n, 2)
                    keep_onehotT(n, 3)
                if f:
                    gate_exps(f)
                messages(6, 7)
            for g in range(G):
                keep_onehotT(Round(act, 0, 0), g)
            for h in range(HALVES):
                act.wait_ge(ld_wr, 16 * HALVES)
                a(wr_r[:, 0, h, :, :], wr[:, h, :, :], ACT.Copy).then_inc(wr_high, 1)
            rounds(act, l0)
            f = Round(act, LAST, 1)
            for h in range(HALVES):
                keep_hT(f, h)
            residual(f)
            deviation(f)
            for c in range(CHUNKS):
                keep_message(Round(act, LAST, 0), c)
            keep_x1T(f)
            gate_exps(f)
            for c in range(CHUNKS):
                keep_message(f, c)

            def l1(f):
                act.wait_ge(l_mv, f.done)
                a(sd[:NODES, :], mv[:NODES, 1:2], ACT.Sqrt, bias=eps[:NODES, :]).then_inc(l_sd, 1)
            rounds(act, l1)

        @block.vector
        def _(dve):
            v = nc.vector
            dve.sem_inc(t_dve, ND)
            dve.wait_ge(ld_grid, 16)
            v.tensor_copy(grid_f[:, :], grid_i[:, :]).then_inc(grid_ready, 1)
            dve.wait_ge(grid_ready, 1)
            for j in range(ROUNDS):
                v.tensor_scalar(grid_o[:, :], grid_f[:, :], float(j * NODES), None, ALU.is_lt, ALU.add,
                                accum_out=cnt[:, j:j + 1]).then_inc(counted, 1)
                dve.wait_ge(counted, j + 1)
            dve.wait_ge(cnt_summed, 1)
            v.tensor_copy(starts[:, :], bank[0][0:1, 0:ROUNDS]).then_inc(starts_ready, 1)

            step = [0]

            def link(ins):
                step[0] += 1
                ins.then_inc(meta_step, 1)
                dve.wait_ge(meta_step, step[0])

            dve.wait_ge(ld_small, 32)
            dve.wait_ge(alpha_exp, 1)
            for t in range(NT):
                link(v.tensor_scalar(nmask[:NODES, 0:ROUNDS, t], nt_i[:NODES, :], float(t), None, ALU.is_equal))
            link(v.tensor_scalar_add(alpha[:, :], alpha[:, :], 1.0))
            link(v.reciprocal(alpha[:, :], alpha[:, :]))
            for t in range(NT):
                link(v.tensor_scalar(calpha[:NODES, :, t], nmask[:NODES, 0:ROUNDS, t], alpha[:NODES, t:t + 1], None, ALU.mult))
            link(v.tensor_reduce(keep[:NODES, :], calpha[:NODES, :, :], AX.X, ALU.add))
            v.tensor_scalar(keep[:NODES, :], keep[:NODES, :], -1.0, 2.0, ALU.mult, ALU.add).then_inc(mask_ready, 1)

            dve.wait_ge(ld_rel, 24 * 16)
            for h in range(HALVES):
                v.scalar_tensor_tensor(rel[:, 0, h, :, :], rel[:, 0, h, :, :], float(D) ** -0.5,
                                       pris[:, h, :].unsqueeze(2).broadcast_to([P, ET, P]),
                                       ALU.mult, ALU.mult).then_inc(rel_ready, 1)
            def low_part(o, i, high):
                return v.tensor_tensor(o, i, high.bitcast(F32), ALU.subtract)

            def make_xm(s):
                for t in range(NT):
                    for q in range(SUPER):
                        j = bass.ds(s * SUPER + (q - SUPER), 1)
                        last = v.tensor_scalar(xm[:, t, q, :], x_all[:, j, :].rearrange("p j c -> p (j c)"),
                                               nmask[:NODES, j, t], None, ALU.mult)
                last.then_inc(xm_ready, 1)

            def keep_xT_low(s, n):
                t, h = TURNS[n]
                dve.wait_ge(x_high, (s - 1) * NX + (n + 1))
                low_part(xmT_r[:, 1, t, h, :], bank[6 + n % 2][:, 0:SN], xmT_r[:, 0, t, h, :]).then_inc(x_low, 1)

            dve.wait_ge(ld_x, 16)
            dve.wait_ge(const_ready, 1)
            make_xm(1)
            for k in range(3):
                dve.wait_ge(w_high, k + 1)
                low_part(w_r[:, 1, k, :, :, :], w_in[:, k, :, :, :], w_r[:, 0, k, :, :, :]).then_inc(w_low, 1)
            dve.wait_ge(gw_high, 1)
            low_part(gw_r[:, 1, :, :], gw[:, :, :], gw_r[:, 0, :, :]).then_inc(gw_low, 1)
            dve.wait_ge(rel_high, 1)
            low_part(rel_r[:, 1, :, :, :, :], rel[:, :, :, :, :], rel_r[:, 0, :, :, :, :]).then_inc(rel_low, 1)
            for n in range(NX):
                keep_xT_low(1, n)
            with dve.Fori(1, STEPS + 1) as s:
                dve.wait_ge(x_filled, s * NX)
                make_xm(s + 1)
                for k, job in enumerate(JOBS):
                    if k in TURN_AT:
                        keep_xT_low(s + 1, TURN_AT[k])
                    if not on_dve(k):
                        continue
                    b = bank[k % JB]
                    if job[0] == "tab":
                        dve.wait_ge(t_filled, s * NJ + (k + 1))
                        o, i = table_part(dve, s, job, b)
                        v.tensor_copy(o, i).then_inc(t_dve, 1)
                        continue
                    dve.wait_ge(t_act, s * NA + A_IDX[k])
                    if job[0] == "kvT":
                        parts, i = [kvT_r[:, k, job[1], job[2], :] for k in range(2)], b[:, 0:SN]
                    else:
                        parts, i = [qstage_r[:, job[1], k, :] for k in range(2)], b[:NODES, 0:C]
                    low_part(parts[1], i, parts[0]).then_inc(t_dve, 1)

            dve.wait_ge(ld_rec, 32 * ROUNDS)
            dve.wait_ge(const_ready, 1)
            field = lambda k: recs[:, :, :, k]
            link(v.tensor_tensor(dstl[:, :, :], field(3), base[:, :].unsqueeze(2).broadcast_to([P, ROUNDS, U]), ALU.subtract))
            for k in range(2):
                link(v.tensor_tensor(same[:, :, k, :], field(3), field(4 + k), ALU.is_equal))
                link(v.tensor_scalar(same[:, :, k, :], same[:, :, k, :], -1.0, BIG, ALU.add, ALU.mult))
            link(v.tensor_copy(edge_mask[:, :, :, :], same[:, :, :, :]))
            link(v.memset(edge_mask[:, :, 0, 0:1], -BIG))
            link(v.memset(edge_mask[:, :, 1, U - 1:U], -BIG))
            for k in range(2):
                link(v.tensor_copy(line[:, 0, :].rearrange("p (j u) -> p j u", u=U), same[:, :, k, :]))
                c = cell[:, k, :, :].rearrange("p j u -> p (j u)")
                if k == 0:
                    link(v.tensor_tensor_scan(line[:, 1, :], c, line[:, 0, :], 0.0, ALU.add, ALU.min))
                else:
                    link(v.tensor_tensor_scan(line[:, 1, ::-1], c[:, ::-1], line[:, 0, ::-1], 0.0, ALU.add, ALU.min))
                link(v.tensor_copy(reach[:, :, k, :], line[:, 1, :].rearrange("p (j u) -> p j u", u=U)))
            link(v.tensor_copy(ends[:, :, 0], reach[:, :, 0, U - 1]))
            link(v.tensor_copy(ends[:, :, 1], reach[:, :, 1, 0]))
            for k, types in enumerate((ET, RT)):
                link(v.scalar_tensor_tensor(rows[:, k, :, :], field(0), float(types), field(1 + k), ALU.mult, ALU.add))
            for k in range(2):
                dve.wait_ge(t_stored[k], 16 * (ROUNDS // 2 + 2))
                dve.wait_ge(q_stored[k], 16 * (ROUNDS // 2 + 2))
            dve.wait_ge(x_low, (STEPS + 1) * NX)
            dve.wait_ge(ident_high, 1)
            v.memset(den[:, :], 1.0).then_inc(tables_over, 1)

            def row_index(r, layer, signal):
                v.tensor_copy(idx[:, r.par, :], rows[:, layer, bass.ds(r.number, 1), :].rearrange("p j u -> p (j u)")
                              ).then_inc(signal[r.par], 1)

            def make_onehot(r, signal, to):
                d = dstl[:, bass.ds(r.number, 1), :].rearrange("p j u -> p (j u)").unsqueeze(2).broadcast_to([P, U, NODES])
                v.tensor_tensor(to[:, r.par, :, :], iota_n[:, :].unsqueeze(1).broadcast_to([P, U, NODES]), d,
                                ALU.is_equal).then_inc(signal, 1)

            def score(r, g):
                dve.wait_ge(kv_landed[r.par][g], r.loads(GU))
                for pr in range(2 * g, 2 * g + 2):
                    dve.wait_ge(qe_ready[pr % 2], r.nth(QB, pr // 2 + 1))
                    k = kv[:, r.par, 2 * pr:2 * pr + 2, 0:C]
                    ins = v.tensor_tensor(k, k, b_qe[pr % 2][:, :].rearrange("p (a c) -> p a c", a=2), ALU.mult)
                    ins.then_inc(qe_used[pr % 2], 1)
                for k in range(2):
                    dve.wait_ge(qe_used[k], r.nth(QB, g + 1))
                for u in range(g * GU, g * GU + GU, 4):
                    v.tensor_reduce(S[:, :, u:u + 4].rearrange("p h u -> p u h"),
                                    kv[:, r.par, u:u + 4, 0:C].rearrange("p u (h d) -> p u h d", h=H),
                                    AX.X, ALU.add).then_inc(scored[g], 1)

            def normalise(f):
                dve.wait_ge(agg_done, f.done)
                v.tensor_scalar_max(den[:NODES, :], b_agg[:NODES, C:C + H], 0.5).then_inc(den_ready, 1)
                dve.wait_ge(den_ready, f.done)
                v.reciprocal(rden[:NODES, :], den[:NODES, :]).then_inc(rden_ready, 1)
                dve.wait_ge(rden_ready, f.done)
                v.tensor_tensor(hN[:NODES, :].rearrange("p (h d) -> p h d", h=H),
                                b_agg[:NODES, 0:C].rearrange("p (h d) -> p h d", h=H),
                                rden[:NODES, :].unsqueeze(2).broadcast_to([NODES, H, D]), ALU.mult).then_inc(hN_ready, 1)
                dve.wait_ge(hN_ready, f.done)
                wait(dve, hT_filled[HALVES - 1], f.number)
                for t in range(NT):
                    last = v.tensor_scalar(hm[:NODES, t, :], hN[:NODES, :], calpha[:NODES, bass.ds(f.number, 1), t],
                                           None, ALU.mult)
                last.then_inc(hm_ready, 1)

            def stats(f):
                dve.wait_ge(wa_done, f.done)
                dve.wait_ge(xs_ready, f.done)
                v.tensor_tensor(z[:NODES, :], z[:NODES, :], b_out[:NODES, 0:C], ALU.add).then_inc(z_ready, 1)
                dve.wait_ge(z_ready, f.done)
                v.bn_stats(st6[:NODES, :], z[:NODES, :]).then_inc(st_ready, 1)
                settle(dve, const_ready)
                dve.wait_ge(st_ready, f.done)
                v.bn_aggr(mv[:NODES, :], st6[:NODES, :]).then_inc(mv_ready, 1)

            def norm_rows(f):
                dve.wait_ge(sd_ready, f.done)
                v.reciprocal(rstd[:NODES, :], sd[:NODES, :]).then_inc(rstd_ready, 1)
                dve.wait_ge(rstd_ready, f.done)
                wait(dve, x1_stored, f.stores_before())
                v.tensor_scalar(x1[:NODES, f.par, :], z[:NODES, :], mv[:NODES, 0:1], rstd[:NODES, 0:1],
                                ALU.subtract, ALU.mult).then_inc(x1_ready, 1)

            def keep_x1T_low(f):
                dve.wait_ge(x1T_high, f.done)
                low_part(x1T_r[:, f.par, 1, :, :], b_x1T.rearrange("p (h n) -> p h n", h=HALVES),
                         x1T_r[:, f.par, 0, :, :]).then_inc(x1T_low, 1)

            def make_gates(f):
                dve.wait_ge(eg_ready, f.done)
                v.tensor_scalar_add(eg1[:NODES, :], eg[:NODES, :], 1.0).then_inc(eg1_ready, 1)
                dve.wait_ge(eg1_ready, f.done)
                v.reciprocal(gate[:NODES, f.par, :], eg1[:NODES, :]).then_inc(gate_ready, 1)

            def softmax(r):
                for g in range(G):
                    dve.wait_ge(scored[g], r.done)
                dve.wait_ge(masks_ready, r.done)
                flat = lambda t: t.rearrange("p h u -> p (h u)")
                v.tensor_tensor_scan(flat(FB[:, 0, :, :]), flat(masks[:, 0, :, :]), flat(S[:, :, :]), -BIG, ALU.add, ALU.max)
                v.tensor_tensor_scan(flat(FB[:, 1, :, :])[:, ::-1], flat(masks[:, 1, :, :])[:, ::-1],
                                     flat(S[:, :, :])[:, ::-1], -BIG, ALU.add, ALU.max).then_inc(scanned, 1)

            def softmax_across(r):
                dve.wait_ge(carry_copied, r.done)
                v.tensor_tensor_scan(carry[:, 0, 1:P + 1], carry_in[:, 1, :], carry_in[:, 0, :], -BIG, ALU.add, ALU.max)
                v.tensor_tensor_scan(carry[:, 1, 0:P][:, ::-1], carry_in[:, 3, :][:, ::-1], carry_in[:, 2, :][:, ::-1],
                                     -BIG, ALU.add, ALU.max).then_inc(carried, 1)

            def softmax_less(r):
                dve.wait_ge(backT, r.done)
                pn = b_tmp[:, 0:2 * H].rearrange("p (k h) -> p k h", k=2).unsqueeze(3).broadcast_to([P, 2, H, U])
                re = reach[:, bass.ds(r.number, 1), :, :].rearrange("p j k u -> p (j k) u").unsqueeze(2).broadcast_to([P, 2, H, U])
                v.tensor_tensor(m2[:, :, :, :], pn, re, ALU.add).then_inc(m_a, 1)
                dve.wait_ge(m_a, r.done)
                v.tensor_tensor(m2[:, :, :, :], m2[:, :, :, :], FB[:, :, :, :], ALU.max).then_inc(m_b, 1)
                dve.wait_ge(m_b, r.done)
                v.tensor_tensor(m2[:, 0, :, :], m2[:, 0, :, :], m2[:, 1, :, :], ALU.max).then_inc(m_c, 1)
                dve.wait_ge(m_c, r.done)
                v.tensor_tensor(S[:, :, :], S[:, :, :], m2[:, 0, :, :], ALU.subtract).then_inc(d_ready, 1)

            def weigh(r):
                dve.wait_ge(ex_ready, r.done)
                for g in range(G):
                    u = slice(g * GU, g * GU + GU)
                    w = kv[:, r.par, u, C:2 * C].rearrange("p u (h d) -> p u h d", h=H)
                    e = kv[:, r.par, u, 2 * C:ROW].unsqueeze(3).broadcast_to([P, GU, H, D])
                    v.tensor_tensor(w, w, e, ALU.mult).then_inc(weighted[g], 1)

            def l0(r):
                f = None if r.first else r.last()
                score(r, 0)
                if r.older:
                    make_gates(r.older)
                score(r, 1)
                if f:
                    normalise(f)
                    if not r.final:
                        row_index(r.next(), 0, idx_ready)
                score(r, 2)
                score(r, 3)
                softmax(r)
                if f:
                    stats(f)
                if not r.final:
                    make_onehot(r.next(), oh_ready, onehot_r)
                softmax_across(r)
                if f:
                    norm_rows(f)
                softmax_less(r)
                weigh(r)
                if f:
                    keep_x1T_low(f)

            row_index(Round(dve, 0, 0), 0, idx_ready)
            row_index(Round(dve, 0, 1), 0, idx_ready)
            make_onehot(Round(dve, 0, 0), oh_ready, onehot_r)
            dve.wait_ge(carry_ends, 1)
            for h in range(HALVES):
                dve.wait_ge(wr_high, h + 1)
                low_part(wr_r[:, 1, h, :, :], wr[:, h, :, :], wr_r[:, 0, h, :, :]).then_inc(wr_low, 1)
            rounds(dve, l0)
            f = Round(dve, LAST, 1)
            normalise(f)
            make_gates(Round(dve, LAST, 0))
            stats(f)
            norm_rows(f)
            keep_x1T_low(f)
            make_gates(f)

            def finish(f):
                wait(dve, l_y, f.number)
                dve.wait_ge(l_agg, f.done)
                dve.wait_ge(l_x[f.par], f.loads(1))
                v.scalar_tensor_tensor(z[:NODES, :], bank[f.par][:NODES, 0:C], 0.0, xb[:NODES, f.par, :],
                                       ALU.max, ALU.add).then_inc(l_z, 1)
                dve.wait_ge(l_z, f.done)
                v.bn_stats(st6[:NODES, :], z[:NODES, :]).then_inc(l_st, 1)
                settle(dve, const_ready)
                dve.wait_ge(l_st, f.done)
                v.bn_aggr(mv[:NODES, :], st6[:NODES, :]).then_inc(l_mv, 1)
                dve.wait_ge(l_sd, f.done)
                v.reciprocal(rstd[:NODES, :], sd[:NODES, :]).then_inc(l_rstd, 1)
                dve.wait_ge(l_rstd, f.done)
                wait(dve, l_out, f.stores_before())
                v.tensor_scalar(x1[:NODES, f.par, :], z[:NODES, :], mv[:NODES, 0:1], rstd[:NODES, 0:1],
                                ALU.subtract, ALU.mult).then_inc(l_y, 1)

            def l1(r):
                wait(dve, l_agg, r.before)
                make_onehot(r, l_oh0, onehot_w)
                dve.wait_ge(l_oh0, r.done)
                w = norms[:, bass.ds(r.number, 1), :].rearrange("p j u -> p (j u)").unsqueeze(2).broadcast_to([P, U, NODES])
                o = onehot_w[:, r.par, :, :]
                v.tensor_tensor(o, o, w, ALU.mult).then_inc(l_oh, 1)
                if not r.first:
                    finish(r.last())
                    if not r.final:
                        row_index(r.next(), 1, l_idx)

            row_index(Round(dve, 0, 0), 1, l_idx)
            row_index(Round(dve, 0, 1), 1, l_idx)
            dve.wait_ge(x1_stored, 16 * ROUNDS)
            dve.wait_ge(m_filled[1], ROUNDS * MB)
            rounds(dve, l1)
            finish(Round(dve, LAST, 1))


def kernel(**inputs):
    import numpy as np
    import concourse.bacc as bacc
    from concourse.bass_utils import run_bass_kernel_spmd

    given = {k: np.asarray(v) for k, v in inputs.items()}
    x = np.zeros((NPAD, C), given["x"].dtype)
    x[:N] = given["x"]
    nt = np.zeros(NPAD, given["node_type_3"].dtype)
    nt[:N] = given["node_type_3"]
    dst = given["dst"]
    rec = np.zeros((EPAD, FIELDS), dst.dtype)
    for k, name in enumerate(("src", "edge_type_5", "edge_type_16")):
        rec[:E, k] = given[name]
    rec[:, 3:] = FAR
    rec[:E, 3] = dst
    rec[0, 4] = -1
    rec[1:E + 1, 4] = dst
    rec[:E - 1, 5] = dst[1:]
    norm = np.zeros(EPAD, given["edge_weight1"].dtype)
    norm[:E] = given["edge_weight1"][:, 0]
    grid = np.full(P * COUNT_COLS, FAR, dst.dtype)
    grid[:E] = dst
    arrays = {
        "x": x, "nt_rows": nt.reshape(ROUNDS, NODES).T, "rec": rec, "norm": norm,
        "dst_grid": grid.reshape(P, COUNT_COLS),
        "Wk": given["L0_gnn_Wk"], "Wq": given["L0_gnn_Wq"], "Wv": given["L0_gnn_Wv"],
        "Ratt": given["L0_gnn_Ratt"], "Rmsg": given["L0_gnn_Rmsg"], "pri": given["L0_gnn_pri"].T,
        "Wa": given["L0_gnn_Wa"], "skip": given["L0_gnn_skip"], "Wr": given["L1_gnn_weight"],
        "gate_w": given["L1_gnn_gate_weight"][:, :, 0].T,
    }
    nc = bacc.Bacc("TRN2", target_bir_lowering=False, num_devices=1)
    sent, args = {}, {}
    for name, a in arrays.items():
        sent[f"in_{name}"] = np.ascontiguousarray(a)
        args[name] = nc.dram_tensor(f"in_{name}", a.shape, mybir.dt.from_np(a.dtype), kind="ExternalInput").ap()
    out = nc.dram_tensor("out", (NPAD, C), F32, kind="ExternalOutput").ap()
    build(nc, out=out, **args)
    result = run_bass_kernel_spmd(nc, [sent], core_ids=[0])
    return result.results[0]["out"][:N]
```

```python
from contextlib import ExitStack

import concourse.bass as bass
from concourse import mybir

F32 = mybir.dt.float32
F32R = mybir.dt.float32r
I32 = mybir.dt.int32
ALU = mybir.AluOpType
ACT = mybir.ActivationFunctionType
AX = mybir.AxisListType

P = 128
C = 256
HALVES = C // P
H, D = 8, 32
NT, ET, RT = 3, 5, 16
N, E = 3125, 50000
NODES = 121
ROUNDS = -(-N // NODES)
U = 16
G, GU = 4, 4
ROUND_EDGES = P * U
EPAD = E + ROUND_EDGES
COUNT_COLS = -(-E // P)
FAR = 1 << 20
BIG = 1e30
ROW = 2 * C + H
SUPER = 4
STEPS = -(-ROUNDS // SUPER)
TILES = STEPS * SUPER
NPAD = TILES * NODES
EPS = 1e-5
CHUNKS = RT // 2
QB = U // 2 // 2
MB = CHUNKS // 2
META = STEPS - 1
EARLY = 4
LAST = ROUNDS // 2 - 1
PARTS = 4
WINDOWS = -(-E // ROUND_EDGES)
EDGES = WINDOWS * ROUND_EDGES
FIELDS = 6


def take(eng, sem, value):
    eng.wait_ge(sem, value)
    eng.sem_clear(sem)


class Round:

    def __init__(self, eng, i, par, again=False):
        self.eng, self.i, self.par = eng, i, par
        self.tile = 2 * i + (par - ROUNDS if again else par)
        self.number = 2 * i + par
        self.done = 2 * i + (par + 1)
        self.before = 2 * i + (par - 1)
        self.first = isinstance(i, int) and self.number == 0
        self.final = isinstance(i, int) and self.number == ROUNDS - 1

    @property
    def older(self):
        return None if isinstance(self.i, int) and self.i == 0 else Round(self.eng, self.i - 1, self.par)

    def nth(self, n, k):
        return self.i * (2 * n) + (self.par * n + k)

    def loads(self, n):
        return self.i * (16 * n) + 16 * n

    def stores_before(self):
        return self.i * 32 + 16 * self.par

    def stores(self):
        return self.i * 32 + 16 * (self.par + 1)

    def last(self):
        return Round(self.eng, self.i, 0) if self.par else Round(self.eng, self.i - 1, 1)

    def next(self):
        return Round(self.eng, self.i, 1) if self.par == 0 else Round(self.eng, self.i + 1, 0)


def settle(eng, sem):
    eng.wait_ge(sem, 1)


def wait(eng, sem, value):
    if not (isinstance(value, int) and value <= 0):
        eng.wait_ge(sem, value)


def build(nc, x, nt_rows, rec, dst_lines, norm, dst_grid, Wk, Wq, Wv, Ratt, Rmsg, pri, Wa, skip, Wr, gate_w, out):
    ktab = nc.dram_tensor("kv_table", [ROUNDS * NODES * ET, 2 * C], F32).ap()
    qtab = nc.dram_tensor("query_table", [ROUNDS * NODES, 2 * C], F32).ap()
    x1tab = nc.dram_tensor("x1_table", [ROUNDS * NODES, C], F32).ap()
    mtab = nc.dram_tensor("message_table", [ROUNDS * NODES * RT, C], F32).ap()
    ktab_n = ktab.rearrange("(n r) c -> n (r c)", r=ET)
    mtab_n = mtab.rearrange("(n r) c -> n (r c)", r=RT)
    scores_d, maxima_d, weights_d = (nc.dram_tensor(n, [H, EDGES], F32).ap()
                                     for n in ("scores_all", "maxima_all", "weights_all"))

    ctx = ExitStack()
    with ctx:
        def sb(name, shape, dt=F32, life=ctx):
            return life.enter_context(nc.sbuf_tensor(name, shape, dt))

        def sem(name):
            return ctx.enter_context(nc.semaphore(name))

        def sems(name, n):
            return [sem(f"{name}{k}") for k in range(n)]

        norms = sb("norms", [P, ROUNDS, U])
        dstl = sb("dstl", [P, ROUNDS, U])
        edge_mask = sb("edge_mask", [P, ROUNDS, 2, U])
        reach = sb("reach", [P, ROUNDS, 2, U])
        ends = sb("ends", [P, ROUNDS, 2])
        rows = sb("rows", [P, 2, ROUNDS, U], I32)
        starts = sb("starts", [1, ROUNDS], I32)
        fill = sb("fill", [1, ROUNDS])
        most = sb("most", [1, 1])
        overfull = sb("overfull", [1, 1], I32)
        ones = sb("ones", [P, 1])
        ident = sb("ident", [P, P])
        ident_r = sb("ident_r", [P, P], F32R)
        iota_n = sb("iota_n", [P, NODES])
        base = sb("base", [P, ROUNDS])
        nmask = sb("nmask", [P, TILES, NT])
        calpha = sb("calpha", [P, ROUNDS, NT])
        keep = sb("keep", [P, ROUNDS])
        alpha = sb("alpha", [P, NT])
        gw = sb("gw", [P, HALVES, RT])
        gw_r = sb("gw_r", [P, 2, HALVES, RT], F32R)
        eps = sb("eps", [P, 1])
        unused = sb("unused", [P, 1])
        idx = sb("idx", [P, 2, U], I32)
        st6 = sb("st6", [P, 6])
        mv = sb("mv", [P, 2])
        sd = sb("sd", [P, 1])
        rstd = sb("rstd", [P, 1])
        den = sb("den", [P, H])
        rden = sb("rden", [P, H])
        gsum = sb("gsum", [P, 2, H])
        eg = sb("eg", [P, RT])
        eg1 = sb("eg1", [P, RT])
        gate = sb("gate", [P, 2, RT])

        SN = SUPER * NODES
        with ExitStack() as t_life:
            def tsb(name, shape, dt=F32):
                return sb(name, shape, dt, t_life)
            w_r = tsb("w_r", [P, 2, 3, NT, HALVES, C], F32R)
            grid_i = tsb("grid_i", [P, COUNT_COLS], I32)
            x_all = tsb("x_all", [NODES, TILES + SUPER, C])
            rel_r = tsb("rel_r", [P, 2, 2, HALVES, ET, P], F32R)
            xm = tsb("xm", [NODES, NT, SUPER, C])
            kvT_r = tsb("kvT_r", [P, 2, 2, HALVES, SN], F32R)
            tstage = tsb("tstage", [NODES, 2, ET, 2 * C])
            qstage_r = tsb("qstage_r", [NODES, SUPER, 2, C], F32R)
            recs = tsb("recs", [P, ROUNDS, U, FIELDS], I32)
            cell = tsb("cell", [P, 2, ROUNDS, U])
            grid_f = tsb("grid_f", [P, COUNT_COLS])
            grid_o = tsb("grid_o", [P, COUNT_COLS])
            cnt = tsb("cnt", [P, ROUNDS])
            with ExitStack() as first_life:
                w_in = sb("w_in", [P, 3, NT, HALVES, C], F32, first_life)
                rel = sb("rel", [P, 2, HALVES, ET, P], F32, first_life)
                pris = sb("pris", [P, HALVES, ET], F32, first_life)
                nt_i = sb("nt_i", [P, TILES], I32, first_life)
                skips = sb("skips", [P, NT], F32, first_life)
            xmT_r = tsb("xmT_r", [P, 2, NT, HALVES, SN], F32R)
            same = tsb("same", [P, ROUNDS, 2, U])
            line = tsb("line", [P, 2, ROUNDS * U])
        with ExitStack() as l_life:
            def lsb(name, shape, dt=F32):
                return sb(name, shape, dt, l_life)
            xb = lsb("xb", [NODES, 2, C])
            x1 = lsb("x1", [NODES, 2, C])
            z = lsb("z", [NODES, C])
            kv = lsb("kv", [P, 2, U, ROW])
            with ExitStack() as m_life:
                def msb(name, shape, dt=F32):
                    return sb(name, shape, dt, m_life)
                wr_r = msb("wr_r", [P, 2, HALVES, RT, C], F32R)
                mstage = msb("mstage", [NODES, 2, RT // PARTS, C])
                wa = msb("wa", [P, NT, HALVES, C])
                onehot_r = msb("onehot_r", [P, 2, U, NODES], F32R)
                onehotT_r = msb("onehotT_r", [NODES, U, P], F32R)
                qb_r = msb("qb_r", [NODES, 2, 2, C], F32R)
                S = msb("S", [P, H, U])
                masks = msb("masks", [P, 2, H, U])
                m2 = masks
                FB = msb("FB", [P, 2, H, U])
                carry_room = msb("carry_room", [P, 4 * P])
                carry_in = carry_room[:H, :].rearrange("p (k n) -> p k n", k=4)
                carry = msb("carry", [H, 2, P + 1])
                hN = z
                hm = msb("hm", [NODES, NT, C])
                hmT = msb("hmT", [P, HALVES, NT, NODES])
                x1T_r = msb("x1T_r", [P, 2, 2, HALVES, NODES], F32R)
            onehot_w = lsb("onehot_w", [P, 2, U, NODES])
        wr = kv[:, 1, :, :].rearrange("p u c -> p (u c)")[:, 0:HALVES * RT * C].rearrange(
            "p (h r c) -> p h r c", h=HALVES, r=RT)

        g_rec_w = FB[:, :, :, :].rearrange("p k h u -> p (k h u)").bitcast(I32)[:, 0:U * FIELDS].rearrange(
            "p (u f) -> p u f", f=FIELDS)
        g_e = masks[:, 0, :, :]
        g_norm = masks[:, 0, 0, :]
        g_local = S[:, 0, :]
        g_acc = carry_room[:NODES, 0:C + H]
        g_lines = kv[:, :, :, :].rearrange("p b u c -> p (b u c)")
        RW = ROUND_EDGES
        g_val, g_mask, g_run = (g_lines[:H, k * (RW + 1):(k + 1) * (RW + 1)] for k in range(3))
        g_here, g_beside, g_score = (g_lines[:H, 3 * (RW + 1) + k * RW:3 * (RW + 1) + (k + 1) * RW] for k in range(3))
        g_here, g_beside = g_here.bitcast(I32), g_beside.bitcast(I32)

        bank = [ctx.enter_context(nc.psum_tensor(f"bank{k}", [P, 512], F32)) for k in range(8)]
        b_x1T = bank[5][:, C:C + HALVES * NODES]
        b_gate = bank[5][:NODES, 0:RT]
        b_qe, b_ohT, b_agg, b_tmp, b_out, b_m = bank[0:2], bank[2], bank[3], bank[4], bank[5], bank[6:8]

        ld_grid, ld_x, ld_wa, ld_wr, ld_gw, ld_rel, ld_small, ld_rec = (sem(n) for n in (
            "ld_grid", "ld_x", "ld_wa", "ld_wr", "ld_gw", "ld_rel", "ld_small", "ld_rec"))
        ld_x0, ld_w, w_high, w_low = sem("ld_x0"), sems("ld_w", 3), sem("w_high"), sem("w_low")
        rel_high, rel_low, wr_high, wr_low, gw_high, gw_low = (sem(n) for n in (
            "rel_high", "rel_low", "wr_high", "wr_low", "gw_high", "gw_low"))
        const_ready, zeroed, rel_ready, ident_high = (sem(n) for n in (
            "const_ready", "zeroed", "rel_ready", "ident_high"))
        pool_step = sem("pool_step")
        counted = sem("counted")
        alpha_exp, grid_ready, meta_step = sem("alpha_exp"), sem("grid_ready"), sem("meta_step")
        cnt_summed, starts_ready, tables_over, mask_ready = (sem(n) for n in (
            "cnt_summed", "starts_ready", "tables_over", "mask_ready"))
        xm_ready, x_filled, x_high, x_low, t_filled, t_act, t_dve = (sem(n) for n in (
            "xm_ready", "x_filled", "x_high", "x_low", "t_filled", "t_act", "t_dve"))
        t_stored, q_stored = sems("t_stored", 2), sems("q_stored", 2)

        q_loaded, x_loaded = sems("q_loaded", 2), sems("x_loaded", 2)
        idx_ready, oh_ready = sems("idx_ready", 2), sem("oh_ready")
        kv_landed = [sems(f"kv_landed{p}_", G) for p in range(2)]
        ohT_filled, ohT_ready = sems("ohT_filled", G), sems("ohT_ready", G)
        qe_ready, qe_used = sems("qe_ready", 2), sems("qe_used", 2)
        scored, carry_ends = sem("scored"), sem("carry_ends")
        masks_ready, scanned, carryT, carry_copied = (sem(n) for n in (
            "masks_ready", "scanned", "carryT", "carry_copied"))
        carried, backT, m_a, m_b, m_c, d_ready, ex_ready = (sem(n) for n in (
            "carried", "backT", "m_a", "m_b", "m_c", "d_ready", "ex_ready"))
        weighted = sems("weighted", G)
        agg_done, table_in = sem("agg_done"), sem("table_in")
        den_ready, rden_ready, hN_ready, hm_ready = (sem(n) for n in (
            "den_ready", "rden_ready", "hN_ready", "hm_ready"))
        hT_filled, hT_ready = sems("hT_filled", HALVES), sems("hT_ready", HALVES)
        wa_done, xs_ready, z_ready, st_ready, mv_ready, sd_ready, rstd_ready, x1_ready = (sem(n) for n in (
            "wa_done", "xs_ready", "z_ready", "st_ready", "mv_ready", "sd_ready", "rstd_ready", "x1_ready"))
        x1T_filled, x1T_high, x1T_low, gate_psum, eg_ready, eg1_ready, gate_ready = (sem(n) for n in (
            "x1T_filled", "x1T_high", "x1T_low", "gate_psum", "eg_ready", "eg1_ready", "gate_ready"))
        m_filled, m_evac = sems("m_filled", 2), sems("m_evac", 2)
        m_stored = sems("m_stored", PARTS)
        x1_stored = sem("x1_stored")

        l_idx, l_oh0, l_oh, l_agg = sems("l_idx", 2), sem("l_oh0"), sem("l_oh"), sem("l_agg")
        l_landed = [sems(f"l_landed{p}_", 2) for p in range(2)]
        l_x = sems("l_x", 2)
        l_z, l_st, l_mv, l_sd, l_rstd, l_y = (sem(n) for n in (
            "l_z", "l_st", "l_mv", "l_sd", "l_rstd", "l_y"))
        l_out = sem("l_out")

        fill_ready, overfull_ready = sem("fill_ready"), sem("overfull_ready")
        g_in, g_idx, g_rows, g_landed, g_scored, g_stored, g_out, g_less, g_exp, g_weighted, g_summed, g_next, g_link = (
            sem("g_" + n) for n in ("in", "idx", "rows", "landed", "scored", "stored", "out", "less", "exp",
                                    "weighted", "summed", "next", "link"))

        block = ctx.enter_context(nc.Block())

        PASSES = ((0, 0), (0, 1), (1, 0))

        class Plan:
            def __init__(self, tiles, last=False):
                self.width = tiles * NODES
                self.jobs = ([("kvT", k, h) for k in range(2) for h in range(HALVES)]
                             + [("q", t) for t in range(tiles)]
                             + [("tab", t, q) for t in range(tiles) for q in range(5)])
                act = [k for k in range(len(self.jobs)) if self.on_act(k)]
                dve = [k for k in range(len(self.jobs)) if self.on_dve(k)]
                self.nth_on_act = {k: n + 1 for n, k in enumerate(act)}
                self.nth_on_dve = {k: n + 1 for n, k in enumerate(dve)}
                self.turns = {} if last else {len(self.jobs) - 18 + 3 * n: n for n in range(NX)}

            def on_act(self, k):
                job = self.jobs[k]
                return job[0] != "tab" or (job[1] + job[2]) % 2 == 0

            def on_dve(self, k):
                return self.jobs[k][0] != "tab" or not self.on_act(k)

            def last_of_tile(self, nth, t):
                return max(n for k, n in nth.items() if self.jobs[k][:2] == ("tab", t))

        TURNS = [(t, h) for t in range(NT) for h in range(HALVES)]
        NX = len(TURNS)
        LEFT = ROUNDS - (STEPS - 1) * SUPER
        full, final = Plan(SUPER), Plan(LEFT, last=True)
        NJ, NA, ND, JB = len(full.jobs), len(full.nth_on_act), len(full.nth_on_dve), 6

        def rounds(eng, body):
            for par in range(2):
                body(Round(eng, 0, par))
            with eng.Fori(1, LAST) as i:
                for par in range(2):
                    body(Round(eng, i, par))
            for par in range(2):
                body(Round(eng, LAST, par))

        def general(eng):
            eng.wait_ge(l_out, 16 * ROUNDS)
            eng.wait_ge(overfull_ready, 1)
            return eng.If(eng.value_load(overfull[0:1, 0:1], min_val=0, max_val=E) > 0)

        def tiles(eng, body):
            with eng.Fori(ROUNDS // 2, ROUNDS) as i:
                for par in range(2):
                    body(Round(eng, i, par, again=True))

        def table_part(eng, s, job, b):
            _, t, q = job
            st = tstage[:NODES, t % 2, :, :]
            eng.wait_ge(t_stored[t % 2], s * 32 + 16 * (t // 2))
            if q < 4:
                return st[:, 0:4, q * P:(q + 1) * P], b[:NODES, :].rearrange("p (r n) -> p r n", r=4)
            return st[:, 4, :], b[:NODES, :]

        @block.sync
        def _(sp):
            for k in range(2):
                sp.sem_inc(t_stored[k], 32)
                sp.sem_inc(q_stored[k], 32)
            sp.dma_start(grid_i[:, :], dst_grid).then_inc(ld_grid, 16)
            x_tiles = x.rearrange("(j p) c -> p j c", p=NODES)
            sp.dma_start(x_all[:, 0:SUPER, :], x_tiles[:, 0:SUPER, :]).then_inc(ld_x0, 16)
            for k, w in enumerate((Wk, Wv, Wq)):
                sp.dma_start(w_in[:, k, :, :, :], w.rearrange("t (h p) n -> p t h n", p=P)).then_inc(ld_w[k], 16)
            sp.wait_ge(zeroed, 1)
            for k, r in enumerate((Ratt, Rmsg)):
                for h in range(H):
                    q = D * (h % 4)
                    sp.dma_start(rel[q:q + D, k, h // 4, :, q:q + D],
                                 r[:, h].rearrange("r d f -> d r f")).then_inc(ld_rel, 16)
            for h in range(H):
                q = D * (h % 4)
                sp.dma_start(pris[q:q + D, h // 4, :], pri[h:h + 1, :].to_broadcast([D, ET])).then_inc(ld_rel, 16)
            sp.dma_start(x_all[:, SUPER:TILES, :], x_tiles[:, SUPER:, :]).then_inc(ld_x, 16)
            def store_tables(s, plan, tiles):
                for t in range(tiles):
                    sp.wait_ge(t_act, s * NA + plan.last_of_tile(plan.nth_on_act, t))
                    sp.dma_start(qtab[bass.ds(s * SN + (t - SUPER) * NODES, NODES), :],
                                 qstage_r[:, t, :, :].rearrange("p k c -> p (k c)").bitcast(F32)).then_inc(q_stored[t % 2], 16)
                    sp.wait_ge(t_dve, s * ND + plan.last_of_tile(plan.nth_on_dve, t))
                    sp.dma_start(ktab_n[bass.ds(s * SN + (t - SUPER) * NODES, NODES), :],
                                 tstage[:, t % 2, :, :].rearrange("p r c -> p (r c)")).then_inc(t_stored[t % 2], 16)
            with sp.Fori(1, STEPS) as s:
                store_tables(s, full, SUPER)
            store_tables(STEPS, final, LEFT)
            sp.wait_ge(tables_over, 1)
            def load(r):
                wait(sp, qe_used[1], r.nth(QB, -QB))
                sp.dma_start(qb_r[:, r.par, :, :].rearrange("p k c -> p (k c)").bitcast(F32),
                             qtab[bass.ds(r.number * NODES, NODES), :]).then_inc(q_loaded[r.par], 16)
                wait(sp, xs_ready, r.before)
                sp.dma_start(xb[:NODES, r.par, :], x[bass.ds(r.number * NODES, NODES), :]).then_inc(x_loaded[r.par], 16)

            def store_x1(f):
                sp.wait_ge(x1_ready, f.done)
                sp.dma_start(x1tab[bass.ds(f.tile * NODES, NODES), :], x1[:NODES, f.par, :]).then_inc(x1_stored, 16)

            def store_messages(f):
                for b in range(PARTS):
                    sp.wait_ge(m_evac[1], f.nth(MB, b + 1 + MB))
                    w = RT // PARTS * C
                    sp.dma_start(mtab_n[bass.ds(f.tile * NODES, NODES), b * w:(b + 1) * w],
                                 mstage[:, b % 2, :, :].rearrange("p r c -> p (r c)")).then_inc(m_stored[b], 16)

            def l0(r):
                if not r.final:
                    load(r.next())
                if r.older:
                    store_messages(r.older)
                if not r.first:
                    store_x1(r.last())
            load(Round(sp, 0, 0))
            sp.dma_start(wa[:, :, :, :], Wa.rearrange("t (h p) n -> p t h n", p=P)).then_inc(ld_wa, 16)
            rounds(sp, l0)
            store_messages(Round(sp, LAST, 0))
            store_x1(Round(sp, LAST, 1))
            store_messages(Round(sp, LAST, 1))
            sp.wait_ge(x1_stored, 16 * ROUNDS)

            def l1(r):
                wait(sp, l_z, r.before)
                sp.dma_start(xb[:NODES, r.par, :], x1tab[bass.ds(r.number * NODES, NODES), :]).then_inc(l_x[r.par], 16)
                if not r.first:
                    last(r.last())

            def last(f):
                sp.wait_ge(l_y, f.done)
                sp.dma_start(out[bass.ds(f.tile * NODES, NODES), :], x1[:NODES, f.par, :]).then_inc(l_out, 16)
            rounds(sp, l1)
            last(Round(sp, LAST, 1))

            with general(sp):
                def window(w):
                    return bass.ds(w * ROUND_EDGES, ROUND_EDGES)

                def load_records(w):
                    sp.dma_start(g_rec_w, rec[window(w), :].rearrange("(p u) f -> p u f", p=P)).then_inc(g_in, 16)

                def store_line(table, w, line):
                    sp.dma_start(table[:, window(w)], line).then_inc(g_stored, 16)
                    take(sp, g_stored, 16)

                def load_neighbours(w, side):
                    for k, to in ((0, g_here), (side, g_beside)):
                        sp.dma_start(to, dst_lines[k:k + 1, window(w)].to_broadcast([H, ROUND_EDGES])
                                     ).then_inc(g_in, 16)

                with sp.Fori(0, WINDOWS) as w:
                    load_records(w)
                    take(sp, g_scored, 1)
                    sp.dma_start(scores_d[:, window(w)].rearrange("h (p u) -> p h u", p=P), S[:, :, :]).then_inc(g_stored, 16)
                    take(sp, g_stored, 16)
                with sp.Fori(0, WINDOWS) as w:
                    load_neighbours(w, 1)
                    sp.dma_start(g_val[:, 1:], scores_d[:, window(w)]).then_inc(g_in, 16)
                    take(sp, g_out, 1)
                    store_line(maxima_d, w, g_run[:, 1:])
                with sp.Fori(0, WINDOWS) as back:
                    w = back * -1 + (WINDOWS - 1)
                    load_neighbours(w, 2)
                    sp.dma_start(g_val[:, 0:RW], maxima_d[:, window(w)]).then_inc(g_in, 16)
                    sp.dma_start(g_score, scores_d[:, window(w)]).then_inc(g_in, 16)
                    take(sp, g_exp, 1)
                    store_line(weights_d, w, g_score)
                for h in range(HALVES):
                    sp.dma_start(wr[:, h, :, :], Wr[:, h * P:(h + 1) * P, :].rearrange("r p n -> p r n")).then_inc(ld_wa, 16)

                def tile0(f):
                    sp.dma_start(xb[:NODES, f.par, :], x[bass.ds(f.tile * NODES, NODES), :]).then_inc(x_loaded[f.par], 16)
                    with sp.Fori(0, WINDOWS) as w:
                        load_records(w)
                        sp.dma_start(g_e, weights_d[:, window(w)].rearrange("h (p u) -> p h u", p=P)).then_inc(g_in, 16)
                        take(sp, g_next, 1)
                    store_x1(f)
                    store_messages(f)
                tiles(sp, tile0)
                sp.wait_ge(x1_stored, 2 * 16 * ROUNDS)

                def tile1(f):
                    sp.dma_start(xb[:NODES, f.par, :], x1tab[bass.ds(f.tile * NODES, NODES), :]).then_inc(l_x[f.par], 16)
                    with sp.Fori(0, WINDOWS) as w:
                        load_records(w)
                        sp.dma_start(g_norm, norm[window(w)].rearrange("(p u) -> p u", p=P)).then_inc(g_in, 16)
                        take(sp, g_next, 1)
                    last(f)
                tiles(sp, tile1)
                sp.wait_ge(l_out, 2 * 16 * ROUNDS)

        @block.gpsimd
        def _(pool):
            pool.memset(rel[:, :, :, :, :], 0.0).then_inc(zeroed, 1)
            pool.memset(ident[:, :], 0.0).then_inc(pool_step, 1)
            pool.memset(ones[:, :], 1.0)
            pool.memset(eps[:, :], EPS)
            pool.memset(cell[:, :, :, :], 0.0).then_inc(pool_step, 1)
            pool.iota(iota_n[:, :], pattern=[[1, NODES]], base=0, channel_multiplier=0,
                      allow_small_or_imprecise_dtypes=True)
            pool.iota(base[:, :], pattern=[[NODES, ROUNDS]], base=0, channel_multiplier=0,
                      allow_small_or_imprecise_dtypes=True)
            pool.wait_ge(pool_step, 2)
            pool.memset(cell[:, 0, :, 0:1], 2 * BIG)
            pool.memset(cell[:, 1, :, U - 1:U], 2 * BIG)
            pool.affine_select(out=ident[:, :], in_=ident[:, :], compare_op=ALU.not_equal, fill=1.0,
                               base=0, pattern=[[-1, P]], channel_multiplier=1).then_inc(const_ready, 1)
            pool.dma_start(nt_i[:NODES, :], nt_rows).then_inc(ld_small, 16)
            pool.dma_start(skips[:, :], skip.rearrange("(a t) -> a t", a=1).to_broadcast([P, NT])).then_inc(ld_small, 16)
            pool.dma_start(gw[:, :, :], gate_w.rearrange("(h p) r -> p h r", p=P)).then_inc(ld_gw, 16)

            pool.wait_ge(starts_ready, 1)
            with pool.Fori(0, ROUNDS) as j:
                s = pool.value_load(starts[0:1, bass.ds(j, 1)], min_val=0, max_val=E)
                pool.dma_start(recs[:, bass.ds(j, 1), :, :].rearrange("p j u f -> p (j u f)"),
                             rec[bass.ds(s, ROUND_EDGES), :].rearrange("(p u) f -> p (u f)", p=P)).then_inc(ld_rec, 16)
                pool.dma_start(norms[:, bass.ds(j, 1), :].rearrange("p j u -> p (j u)"),
                             norm[bass.ds(s, ROUND_EDGES)].rearrange("(p u) -> p u", p=P)).then_inc(ld_rec, 16)

            pool.wait_ge(xm_ready, STEPS)
            for h in range(HALVES):
                pool.dma_start(wr[:, h, :, :], Wr[:, h * P:(h + 1) * P, :].rearrange("r p n -> p r n")).then_inc(ld_wr, 16)
            pool.wait_ge(tables_over, 1)
            pool.memset(carry[:, 0, 0:1], -BIG)
            pool.memset(carry[:, 1, P:P + 1], -BIG).then_inc(carry_ends, 1)

            def gather(pair, table, width, indices, landed):
                for par in range(2):
                    settle(pool, const_ready)
                    if isinstance(pair, int) and par == 1 and table is ktab:
                        pool.wait_ge(wr_low, HALVES)
                    pool.wait_ge(indices[par], pair)
                    for u in range(U):
                        pool.indirect_dma_start(kv[:, par, u, 0:width], None, table,
                                                bass.IndirectOffsetOnAxis(ap=idx[:, par, u:u + 1], axis=0)
                                                ).then_inc(landed[par][u * len(landed[par]) // U], 16)

            gather(1, ktab, 2 * C, idx_ready, kv_landed)
            with pool.Fori(2, ROUNDS // 2 + 1) as pair:
                gather(pair, ktab, 2 * C, idx_ready, kv_landed)
            for b in range(PARTS):
                pool.wait_ge(m_stored[b], 16 * (ROUNDS + 1))
            pool.wait_ge(agg_done, ROUNDS)

            with pool.Fori(1, ROUNDS // 2 + 1) as pair:
                gather(pair, mtab, C, l_idx, l_landed)

            with general(pool):
                def gather_window(table, width, b=0):
                    for u in range(U):
                        pool.indirect_dma_start(kv[:, b, u, 0:width], None, table,
                                                bass.IndirectOffsetOnAxis(ap=idx[:, b, u:u + 1], axis=0)
                                                ).then_inc(g_rows, 16)

                def pass_on(gathers):
                    pool.wait_ge(g_rows, gathers * 16)
                    pool.dma_reset(range(g_rows.num, g_rows.num + 1))
                    pool.sem_clear(g_rows)
                    pool.sem_inc(g_landed, 1)
                with pool.Fori(0, WINDOWS):
                    take(pool, g_idx, 1)
                    gather_window(ktab, 2 * C)
                    gather_window(qtab, 2 * C, 1)
                    pass_on(2 * U)
                for table, width in ((ktab, 2 * C), (mtab, C)):
                    with pool.Fori(0, ROUNDS * WINDOWS):
                        take(pool, g_idx, 1)
                        gather_window(table, width)
                        pass_on(U)

        @block.tensor
        def _(pe):
            mm = nc.tensor.matmul
            pe.sem_inc(t_filled, NJ)
            pe.wait_ge(const_ready, 1)

            def turn_x(s, n):
                t, h = TURNS[n]
                b = bank[6 + n % 2]
                if n == 0:
                    pe.wait_ge(xm_ready, s)
                wait(pe, x_low, (s - 1) * NX + (n - 1))
                for q in range(SUPER):
                    last = nc.tensor.transpose(b[:, q * NODES:(q + 1) * NODES],
                                               xm[:, t, q, h * P:(h + 1) * P], ident[:NODES, :NODES])
                last.then_inc(x_filled, 1)

            for n in range(NX):
                turn_x(1, n)
            pe.wait_ge(w_high, 3)
            pe.wait_ge(w_low, 3)
            pe.wait_ge(rel_high, 1)
            pe.wait_ge(rel_low, 1)

            def table_step(s, plan=full):
                pe.wait_ge(x_high, s * NX)
                pe.wait_ge(x_low, s * NX)
                for k, job in enumerate(plan.jobs):
                    if k in plan.turns:
                        turn_x(s + 1, plan.turns[k])
                    b = bank[k % JB]
                    before, of, there = (s, plan, k - JB) if k >= JB else (s - 1, full, max(j for j in range(NJ) if j % JB == k))
                    if of.on_dve(there):
                        pe.wait_ge(t_dve, before * ND + of.nth_on_dve[there])
                    else:
                        pe.wait_ge(t_act, before * NA + of.nth_on_act[there])
                    if job[0] == "kvT":
                        _, kk, ho = job
                        terms = [(w_r[:, a, kk, t, h, ho * P:(ho + 1) * P], xmT_r[:, c, t, h, 0:plan.width])
                                 for t in range(NT) for h in range(HALVES) for a, c in PASSES]
                        for n, (lhsT, rhs) in enumerate(terms):
                            last = mm(b[:, 0:plan.width], lhsT, rhs, start=(n == 0), stop=(n == len(terms) - 1))
                    elif job[0] == "q":
                        o = slice(job[1] * NODES, (job[1] + 1) * NODES)
                        terms = [(xmT_r[:, a, t, h, o], w_r[:, c, 2, t, h, :])
                                 for t in range(NT) for h in range(HALVES) for a, c in PASSES]
                        for n, (lhsT, rhs) in enumerate(terms):
                            last = mm(b[:NODES, 0:C], lhsT, rhs, start=(n == 0), stop=(n == len(terms) - 1))
                    else:
                        _, t, q = job
                        o = slice(t * NODES, (t + 1) * NODES)
                        if (t, q) == (0, 0):
                            last_kv = plan.jobs.index(("kvT", 1, HALVES - 1))
                            pe.wait_ge(t_act, s * NA + plan.nth_on_act[last_kv])
                            pe.wait_ge(t_dve, s * ND + plan.nth_on_dve[last_kv])
                        if q < 4:
                            kk, h = q // 2, q % 2
                            for n, (a, c) in enumerate(PASSES):
                                last = mm(b[:NODES, 0:4 * P], kvT_r[:, a, kk, h, o], rel_r[:, c, kk, h, 0:4, :],
                                          start=(n == 0), stop=(n == 2))
                        else:
                            for kk in range(2):
                                for h in range(2):
                                    z0 = (2 * kk + h) * P
                                    for n, (a, c) in enumerate(PASSES):
                                        last = mm(b[:NODES, z0:z0 + P], kvT_r[:, a, kk, h, o], rel_r[:, c, kk, h, 4, :],
                                                  start=(n == 0), stop=(n == 2))
                    last.then_inc(t_filled, 1)

            table_step(1)
            pe.wait_ge(counted, ROUNDS)
            pe.wait_ge(t_act, 2 * NA)
            pe.wait_ge(t_dve, 2 * ND)
            mm(bank[0][0:1, 0:ROUNDS], ones[:, :], cnt[:, :], start=True, stop=True).then_inc(cnt_summed, 1)
            pe.wait_ge(starts_ready, 1)
            with pe.Fori(2, STEPS) as s:
                table_step(s)
            table_step(STEPS, final)
            pe.wait_ge(tables_over, 1)
            pe.wait_ge(gw_high, 1)
            pe.wait_ge(gw_low, 1)

            def turn_onehot(r, g):
                if g == 0:
                    pe.wait_ge(oh_ready, r.done)
                if g:
                    pe.wait_ge(ohT_ready[g - 1], r.done)
                else:
                    wait(pe, ohT_ready[G - 1], r.number)
                for q in range(GU):
                    last = mm(b_ohT[:NODES, q * P:(q + 1) * P], onehot_r[:, r.par, g * GU + q, :], ident_r[:, :],
                              start=True, stop=True)
                last.then_inc(ohT_filled[g], 1)

            def hand_queries(r, g):
                if g == 0:
                    pe.wait_ge(q_loaded[r.par], r.loads(1))
                pe.wait_ge(ohT_ready[g], r.done)
                for pr in range(2 * g, 2 * g + 2):
                    wait(pe, qe_used[pr % 2], r.nth(QB, pr // 2))
                    for q in range(2):
                        for part in range(2):
                            last = mm(b_qe[pr % 2][:, q * C:(q + 1) * C], onehotT_r[:, 2 * pr + q, :],
                                      qb_r[:, r.par, part, :], start=(part == 0), stop=(part == 1))
                    last.then_inc(qe_ready[pr % 2], 1)

            def turn_h(f, h):
                if h == 0:
                    pe.wait_ge(hm_ready, f.done)
                else:
                    pe.wait_ge(hT_ready[h - 1], f.done)
                for t in range(NT):
                    last = nc.tensor.transpose(b_tmp[:, t * NODES:(t + 1) * NODES],
                                               hm[:NODES, t, h * P:(h + 1) * P], ident[:NODES, :NODES])
                last.then_inc(hT_filled[h], 1)

            def project(f):
                for h in range(HALVES):
                    pe.wait_ge(hT_ready[h], f.done)
                for n, (h, t) in enumerate((h, t) for h in range(HALVES) for t in range(NT)):
                    last = mm(b_out[:NODES, 0:C], hmT[:, h, t, :], wa[:, t, h, :],
                              start=(n == 0), stop=(n == 2 * NT - 1))
                last.then_inc(wa_done, 1)

            def turn_x1(f):
                pe.wait_ge(x1_ready, f.done)
                for h in range(HALVES):
                    last = nc.tensor.transpose(b_x1T[:, h * NODES:(h + 1) * NODES],
                                               x1[:NODES, f.par, h * P:(h + 1) * P], ident[:NODES, :NODES])
                last.then_inc(x1T_filled, 1)

            def gates(f):
                pe.wait_ge(x1T_high, f.done)
                pe.wait_ge(x1T_low, f.done)
                terms = [(h, a, c) for h in range(HALVES) for a, c in PASSES]
                for n, (h, a, c) in enumerate(terms):
                    last = mm(b_gate, x1T_r[:, f.par, a, h, :], gw_r[:, c, h, :],
                              start=(n == 0), stop=(n == len(terms) - 1))
                last.then_inc(gate_psum, 1)

            def message(f, c):
                pe.wait_ge(m_evac[c % 2], f.nth(MB, c // 2 + MB))
                terms = [(h, a, w) for h in range(HALVES) for a, w in PASSES]
                for n, (h, a, w) in enumerate(terms):
                    last = mm(b_m[c % 2][:NODES, :], x1T_r[:, f.par, a, h, :], wr_r[:, w, h, 2 * c:2 * c + 2, :],
                              start=(n == 0), stop=(n == len(terms) - 1))
                last.then_inc(m_filled[c % 2], 1)

            def turn_carry(r):
                pe.wait_ge(scanned, r.done)
                pe.wait_ge(masks_ready, r.done)
                for k, a in enumerate((FB[:, 0, :, U - 1], gsum[:, 0, :], FB[:, 1, :, 0], gsum[:, 1, :])):
                    last = nc.tensor.transpose(b_tmp[:H, k * P:(k + 1) * P], a, ident[:, :])
                last.then_inc(carryT, 1)

            def turn_back(r):
                settle(pe, const_ready)
                pe.wait_ge(carried, r.done)
                nc.tensor.transpose(b_tmp[:, 0:H], carry[:, 0, 0:P], ident[:H, :H])
                nc.tensor.transpose(b_tmp[:, H:2 * H], carry[:, 1, 1:P + 1],
                                    ident[:H, :H]).then_inc(backT, 1)

            def aggregate(r, g):
                pe.wait_ge(weighted[g], r.done)
                if g == 0:
                    wait(pe, hN_ready, r.number)
                for u in range(g * GU, g * GU + GU):
                    last = mm(b_agg[:NODES, 0:C + H], onehot_r[:, r.par, u, :].bitcast(F32), kv[:, r.par, u, C:ROW],
                              start=(u == 0), stop=(u == U - 1))
                if g == G - 1:
                    last.then_inc(agg_done, 1)

            def l0(r):
                f = None if r.first else r.last()

                def messages(*chunks):
                    if r.older:
                        for c in chunks:
                            message(r.older, c)
                n = None if r.final else r.next()
                if f:
                    turn_h(f, 0)
                messages(0)
                hand_queries(r, 3)
                if f:
                    turn_h(f, 1)
                messages(1)
                if f:
                    project(f)
                turn_carry(r)
                if r.first:
                    pe.wait_ge(wr_high, HALVES)
                    pe.wait_ge(wr_low, HALVES)
                messages(2, 3)
                turn_back(r)
                if n:
                    turn_onehot(n, 0)
                messages(4)
                if n:
                    turn_onehot(n, 1)
                    hand_queries(n, 0)
                if f:
                    turn_x1(f)
                messages(5)
                aggregate(r, 0)
                aggregate(r, 1)
                if n:
                    turn_onehot(n, 2)
                    hand_queries(n, 1)
                if f:
                    gates(f)
                aggregate(r, 2)
                if n:
                    turn_onehot(n, 3)
                aggregate(r, 3)
                if n:
                    hand_queries(n, 2)
                messages(6, 7)

            first = Round(pe, 0, 0)
            for g in range(G):
                turn_onehot(first, g)
            for g in range(G - 1):
                hand_queries(first, g)
            pe.wait_ge(ld_wa, 16)
            rounds(pe, l0)
            o, f = Round(pe, LAST, 0), Round(pe, LAST, 1)
            message(o, 0)
            turn_h(f, 0)
            message(o, 1)
            turn_h(f, 1)
            message(o, 2)
            project(f)
            for c in range(3, 6):
                message(o, c)
            turn_x1(f)
            message(o, 6)
            message(o, 7)
            gates(f)
            for c in range(CHUNKS):
                message(f, c)

            def l1(r):
                wait(pe, l_z, r.before)
                pe.wait_ge(l_oh, r.done)
                for u in range(U):
                    if u % (U // 2) == 0:
                        pe.wait_ge(l_landed[r.par][u * 2 // U], r.loads(U // 2))
                    last = mm(bank[r.par][:NODES, 0:C], onehot_w[:, r.par, u, :], kv[:, r.par, u, 0:C],
                              start=(u == 0), stop=(u == U - 1))
                last.then_inc(l_agg, 1)
            pe.wait_ge(qe_used[1], ROUNDS * QB)
            rounds(pe, l1)

            with general(pe):
                def sum_windows(hot, rows):
                    with pe.Fori(0, WINDOWS):
                        take(pe, g_weighted, 1)
                        for u in range(U):
                            last = mm(b_agg[:NODES, 0:rows.stop - rows.start], hot(u), kv[:, 0, u, rows],
                                      start=(u == 0), stop=(u == U - 1))
                        last.then_inc(g_summed, 1)

                pe.wait_ge(wr_high, 2 * HALVES)
                pe.wait_ge(wr_low, 2 * HALVES)

                def tile0(f):
                    sum_windows(lambda u: onehot_r[:, 0, u, :].bitcast(F32), slice(C, ROW))
                    for h in range(HALVES):
                        turn_h(f, h)
                    project(f)
                    turn_x1(f)
                    gates(f)
                    for c in range(CHUNKS):
                        message(f, c)
                tiles(pe, tile0)
                tiles(pe, lambda f: sum_windows(lambda u: onehot_w[:, 0, u, :], slice(0, C)))

        @block.scalar
        def _(act):
            a = nc.scalar.activation
            act.sem_inc(t_act, NA)
            for k in range(2):
                act.sem_inc(m_evac[k], MB)
            for b in range(PARTS):
                act.sem_inc(m_stored[b], 16)
            act.wait_ge(ld_small, 32)
            a(alpha[:, :], skips[:, :], ACT.Exp, scale=-1.0).then_inc(alpha_exp, 1)
            for k in range(3):
                act.wait_ge(ld_w[k], 16)
                a(w_r[:, 0, k, :, :, :], w_in[:, k, :, :, :], ACT.Copy).then_inc(w_high, 1)
            act.wait_ge(const_ready, 1)
            a(ident_r[:, :], ident[:, :], ACT.Copy).then_inc(ident_high, 1)
            act.wait_ge(ld_gw, 16)
            a(gw_r[:, 0, :, :], gw[:, :, :], ACT.Copy).then_inc(gw_high, 1)
            act.wait_ge(rel_ready, HALVES)
            a(rel_r[:, 0, :, :, :, :], rel[:, :, :, :, :], ACT.Copy).then_inc(rel_high, 1)

            def keep_xT(s, n):
                t, h = TURNS[n]
                act.wait_ge(x_filled, (s - 1) * NX + (n + 1))
                a(xmT_r[:, 0, t, h, :], bank[6 + n % 2][:, 0:SN], ACT.Copy).then_inc(x_high, 1)

            act.wait_ge(w_low, 3)
            act.wait_ge(rel_low, 1)
            act.wait_ge(mask_ready, 1)
            for n in range(NX):
                keep_xT(1, n)
            def table_step(s, plan=full):
                for k, job in enumerate(plan.jobs):
                    if k in plan.turns:
                        keep_xT(s + 1, plan.turns[k])
                    if not plan.on_act(k):
                        continue
                    act.wait_ge(t_filled, s * NJ + (k + 1))
                    b = bank[k % JB]
                    if job[0] == "kvT":
                        o, i = kvT_r[:, 0, job[1], job[2], 0:plan.width], b[:, 0:plan.width]
                    elif job[0] == "q":
                        t = job[1]
                        act.wait_ge(q_stored[t % 2], s * 32)
                        o, i = qstage_r[:, t, 0, :], b[:NODES, 0:C]
                    else:
                        o, i = table_part(act, s, job, b)
                    a(o, i, ACT.Copy).then_inc(t_act, 1)
            with act.Fori(1, STEPS) as s:
                table_step(s)
            table_step(STEPS, final)
            act.wait_ge(tables_over, 1)

            def spread_masks(r):
                wait(act, d_ready, r.number)
                j = bass.ds(r.number, 1)
                a(masks[:, :, :, :], edge_mask[:, j, :, :].rearrange("p j k u -> p (j k) u").unsqueeze(2)
                  .broadcast_to([P, 2, H, U]), ACT.Copy)
                a(gsum[:, :, :], ends[:, j, :].rearrange("p j k -> p (j k)").unsqueeze(2)
                  .broadcast_to([P, 2, H]), ACT.Copy).then_inc(masks_ready, 1)

            def keep_onehotT(r, g):
                act.wait_ge(ohT_filled[g], r.done)
                a(onehotT_r[:, g * GU:(g + 1) * GU, :], b_ohT[:NODES, :].rearrange("p (a b) -> p a b", a=GU),
                  ACT.Copy).then_inc(ohT_ready[g], 1)

            def keep_hT(f, h):
                act.wait_ge(hT_filled[h], f.done)
                a(hmT[:, h, :, :], b_tmp[:, 0:NT * NODES].rearrange("p (t n) -> p t n", t=NT),
                  ACT.Copy).then_inc(hT_ready[h], 1)

            def residual(f):
                act.wait_ge(x_loaded[f.par], f.loads(1))
                wait(act, x1_ready, f.number)
                a(z[:, :], xb[:NODES, f.par, :], ACT.Copy,
                  scale=keep[:NODES, bass.ds(f.tile, 1)]).then_inc(xs_ready, 1)

            def deviation(f):
                act.wait_ge(mv_ready, f.done)
                a(sd[:NODES, :], mv[:NODES, 1:2], ACT.Sqrt, bias=eps[:NODES, :]).then_inc(sd_ready, 1)
                wait(act, table_in, f.number)
                a(unused[:, :], eps[:, :], ACT.Exp).then_inc(table_in, 1)

            def keep_x1T(f):
                act.wait_ge(x1T_filled, f.done)
                a(x1T_r[:, f.par, 0, :, :], b_x1T.rearrange("p (h n) -> p h n", h=HALVES),
                  ACT.Copy).then_inc(x1T_high, 1)

            def gate_exps(f):
                act.wait_ge(gate_psum, f.done)
                a(eg[:NODES, :], b_gate, ACT.Exp, scale=-1.0).then_inc(eg_ready, 1)

            def keep_message(f, c):
                b = c * PARTS // CHUNKS
                if c == 0:
                    act.wait_ge(gate_ready, f.done)
                if c % (CHUNKS // PARTS) == 0:
                    if b < 2:
                        act.wait_ge(m_stored[b + 2], f.stores_before() + 16)
                    else:
                        act.wait_ge(m_stored[b - 2], f.stores() + 16)
                act.wait_ge(m_filled[c % 2], f.nth(MB, c // 2 + 1))
                for k in range(2):
                    q = 2 * c + k
                    last = a(mstage[:, b % 2, q % (RT // PARTS), :], b_m[c % 2][:NODES, k * C:(k + 1) * C],
                             ACT.Copy, scale=gate[:NODES, f.par, q:q + 1])
                last.then_inc(m_evac[c % 2], 1)

            def keep_carry(r):
                act.wait_ge(carryT, r.done)
                a(carry_in, b_tmp[:H, :].rearrange("p (k n) -> p k n", k=4), ACT.Copy).then_inc(carry_copied, 1)

            def exps(r):
                act.wait_ge(d_ready, r.done)
                a(kv[:, r.par, :, 2 * C:ROW], S[:, :, :].rearrange("p h u -> p u h"), ACT.Exp).then_inc(ex_ready, 1)

            act.wait_ge(mask_ready, 1)

            def l0(r):
                f = None if r.first else r.last()

                def messages(*chunks):
                    if r.older:
                        for c in chunks:
                            keep_message(r.older, c)
                n = None if r.final else r.next()
                spread_masks(r)
                if f:
                    keep_hT(f, 0)
                messages(0)
                if f:
                    keep_hT(f, 1)
                    residual(f)
                messages(1)
                keep_carry(r)
                if f:
                    deviation(f)
                messages(2)
                messages(3)
                if n:
                    keep_onehotT(n, 0)
                exps(r)
                if n:
                    keep_onehotT(n, 1)
                messages(4)
                if f:
                    keep_x1T(f)
                messages(5)
                if n:
                    keep_onehotT(n, 2)
                if f:
                    gate_exps(f)
                if n:
                    keep_onehotT(n, 3)
                messages(6, 7)
            act.wait_ge(ld_wr, 16 * HALVES)
            for g in range(G):
                keep_onehotT(Round(act, 0, 0), g)
                if g % 2 == 0:
                    a(wr_r[:, 0, g // 2, :, :], wr[:, g // 2, :, :], ACT.Copy).then_inc(wr_high, 1)
            rounds(act, l0)
            o, f = Round(act, LAST, 0), Round(act, LAST, 1)
            keep_message(o, 0)
            keep_hT(f, 0)
            keep_message(o, 1)
            keep_hT(f, 1)
            residual(f)
            keep_message(o, 2)
            keep_message(o, 3)
            deviation(f)
            keep_message(o, 4)
            keep_message(o, 5)
            keep_x1T(f)
            keep_message(o, 6)
            keep_message(o, 7)
            gate_exps(f)
            for c in range(CHUNKS):
                keep_message(f, c)

            def l1(f):
                act.wait_ge(l_mv, f.done)
                a(sd[:NODES, :], mv[:NODES, 1:2], ACT.Sqrt, bias=eps[:NODES, :]).then_inc(l_sd, 1)
            rounds(act, l1)

            with general(act):
                with act.Fori(0, WINDOWS):
                    take(act, g_less, 1)
                    a(g_score, g_score, ACT.Exp).then_inc(g_exp, 1)
                for h in range(HALVES):
                    act.wait_ge(ld_wa, 16 * (1 + HALVES))
                    a(wr_r[:, 0, h, :, :], wr[:, h, :, :], ACT.Copy).then_inc(wr_high, 1)

                def tile0(f):
                    for h in range(HALVES):
                        keep_hT(f, h)
                    residual(f)
                    deviation(f)
                    keep_x1T(f)
                    gate_exps(f)
                    for c in range(CHUNKS):
                        keep_message(f, c)
                tiles(act, tile0)
                tiles(act, l1)

        @block.vector
        def _(dve):
            v = nc.vector
            dve.sem_inc(t_dve, ND)
            dve.wait_ge(ld_grid, 16)
            v.tensor_copy(grid_f[:, :], grid_i[:, :]).then_inc(grid_ready, 1)
            dve.wait_ge(grid_ready, 1)

            def count(tiles):
                for j in tiles:
                    v.tensor_scalar(grid_o[:, :], grid_f[:, :], float(j * NODES), None, ALU.is_lt, ALU.add,
                                    accum_out=cnt[:, j:j + 1]).then_inc(counted, 1)
                    dve.wait_ge(counted, j + 1)

            step = [0]

            def link(ins):
                step[0] += 1
                ins.then_inc(meta_step, 1)
                dve.wait_ge(meta_step, step[0])

            count(range(EARLY))
            dve.wait_ge(ld_small, 32)
            dve.wait_ge(alpha_exp, 1)
            for t in range(NT):
                link(v.tensor_scalar(nmask[:NODES, 0:TILES, t], nt_i[:NODES, :], float(t), None, ALU.is_equal))
            link(v.tensor_scalar_add(alpha[:, :], alpha[:, :], 1.0))
            link(v.reciprocal(alpha[:, :], alpha[:, :]))
            for t in range(NT):
                link(v.tensor_scalar(calpha[:NODES, :, t], nmask[:NODES, 0:ROUNDS, t], alpha[:NODES, t:t + 1], None, ALU.mult))
            link(v.tensor_reduce(keep[:NODES, :], calpha[:NODES, :, :], AX.X, ALU.add))
            v.tensor_scalar(keep[:NODES, :], keep[:NODES, :], -1.0, 2.0, ALU.mult, ALU.add).then_inc(mask_ready, 1)

            def low_part(o, i, high):
                return v.tensor_tensor(o, i, high.bitcast(F32), ALU.subtract)

            def make_xm(s):
                for t in range(NT):
                    for q in range(SUPER):
                        j = bass.ds(s * SUPER + (q - SUPER), 1)
                        last = v.tensor_scalar(xm[:, t, q, :], x_all[:, j, :].rearrange("p j c -> p (j c)"),
                                               nmask[:NODES, j, t], None, ALU.mult)
                last.then_inc(xm_ready, 1)

            def keep_xT_low(s, n):
                t, h = TURNS[n]
                dve.wait_ge(x_high, (s - 1) * NX + (n + 1))
                low_part(xmT_r[:, 1, t, h, :], bank[6 + n % 2][:, 0:SN], xmT_r[:, 0, t, h, :]).then_inc(x_low, 1)

            dve.wait_ge(ld_x0, 16)
            dve.wait_ge(const_ready, 1)
            make_xm(1)
            for k in range(3):
                dve.wait_ge(w_high, k + 1)
                low_part(w_r[:, 1, k, :, :, :], w_in[:, k, :, :, :], w_r[:, 0, k, :, :, :]).then_inc(w_low, 1)
            dve.wait_ge(ld_rel, 24 * 16)
            for h in range(HALVES):
                v.scalar_tensor_tensor(rel[:, 0, h, :, :], rel[:, 0, h, :, :], float(D) ** -0.5,
                                       pris[:, h, :].unsqueeze(2).broadcast_to([P, ET, P]),
                                       ALU.mult, ALU.mult).then_inc(rel_ready, 1)
            dve.wait_ge(gw_high, 1)
            low_part(gw_r[:, 1, :, :], gw[:, :, :], gw_r[:, 0, :, :]).then_inc(gw_low, 1)
            dve.wait_ge(rel_high, 1)
            low_part(rel_r[:, 1, :, :, :, :], rel[:, :, :, :, :], rel_r[:, 0, :, :, :, :]).then_inc(rel_low, 1)
            for n in range(NX):
                keep_xT_low(1, n)
            count(range(EARLY, ROUNDS))
            dve.wait_ge(ld_x, 16)

            def table_step(s, plan=full):
                if plan is full:
                    dve.wait_ge(x_filled, s * NX)
                    make_xm(s + 1)
                for k, job in enumerate(plan.jobs):
                    if k in plan.turns:
                        keep_xT_low(s + 1, plan.turns[k])
                    if not plan.on_dve(k):
                        continue
                    b = bank[k % JB]
                    if job[0] == "tab":
                        dve.wait_ge(t_filled, s * NJ + (k + 1))
                        o, i = table_part(dve, s, job, b)
                        v.tensor_copy(o, i).then_inc(t_dve, 1)
                        continue
                    dve.wait_ge(t_act, s * NA + plan.nth_on_act[k])
                    if job[0] == "kvT":
                        parts, i = [kvT_r[:, part, job[1], job[2], 0:plan.width] for part in range(2)], b[:, 0:plan.width]
                    else:
                        parts, i = [qstage_r[:, job[1], part, :] for part in range(2)], b[:NODES, 0:C]
                    low_part(parts[1], i, parts[0]).then_inc(t_dve, 1)

            table_step(1)
            dve.wait_ge(cnt_summed, 1)
            v.tensor_copy(starts[:, :], bank[0][0:1, 0:ROUNDS]).then_inc(starts_ready, 1)
            dve.wait_ge(starts_ready, 1)
            v.tensor_scalar(fill[:, ROUNDS - 1:], starts[:, ROUNDS - 1:], -1.0, float(E), ALU.mult, ALU.add)
            v.tensor_tensor(fill[:, 0:ROUNDS - 1], starts[:, 1:], starts[:, 0:ROUNDS - 1], ALU.subtract).then_inc(fill_ready, 1)
            dve.wait_ge(fill_ready, 1)
            v.tensor_reduce(most[:, :], fill[:, :], AX.X, ALU.max).then_inc(fill_ready, 1)
            dve.wait_ge(fill_ready, 2)
            v.tensor_scalar(overfull[:, :], most[:, :], -float(ROUND_EDGES), 0.0, ALU.add, ALU.max).then_inc(overfull_ready, 1)
            with dve.Fori(2, META) as s:
                table_step(s)

            dve.wait_ge(ld_rec, 32 * ROUNDS)
            dve.wait_ge(const_ready, 1)
            field = lambda k: recs[:, :, :, k]
            link(v.tensor_tensor(dstl[:, :, :], field(3), base[:, :].unsqueeze(2).broadcast_to([P, ROUNDS, U]), ALU.subtract))
            for k in range(2):
                link(v.tensor_tensor(same[:, :, k, :], field(3), field(4 + k), ALU.is_equal))
                link(v.tensor_scalar(same[:, :, k, :], same[:, :, k, :], -1.0, BIG, ALU.add, ALU.mult))
            link(v.tensor_copy(edge_mask[:, :, :, :], same[:, :, :, :]))
            link(v.memset(edge_mask[:, :, 0, 0:1], -BIG))
            link(v.memset(edge_mask[:, :, 1, U - 1:U], -BIG))
            for k in range(2):
                link(v.tensor_copy(line[:, 0, :].rearrange("p (j u) -> p j u", u=U), same[:, :, k, :]))
                c = cell[:, k, :, :].rearrange("p j u -> p (j u)")
                if k == 0:
                    link(v.tensor_tensor_scan(line[:, 1, :], c, line[:, 0, :], 0.0, ALU.add, ALU.min))
                else:
                    link(v.tensor_tensor_scan(line[:, 1, ::-1], c[:, ::-1], line[:, 0, ::-1], 0.0, ALU.add, ALU.min))
                link(v.tensor_copy(reach[:, :, k, :], line[:, 1, :].rearrange("p (j u) -> p j u", u=U)))
            link(v.tensor_copy(ends[:, :, 0], reach[:, :, 0, U - 1]))
            link(v.tensor_copy(ends[:, :, 1], reach[:, :, 1, 0]))
            for k, types in enumerate((ET, RT)):
                link(v.scalar_tensor_tensor(rows[:, k, :, :], field(0), float(types), field(1 + k), ALU.mult, ALU.add))
            with dve.Fori(META, STEPS) as s:
                table_step(s)
            table_step(STEPS, final)
            for k in range(2):
                dve.wait_ge(t_stored[k], 16 * (ROUNDS // 2 + 2))
                dve.wait_ge(q_stored[k], 16 * (ROUNDS // 2 + 2))
            dve.wait_ge(x_low, STEPS * NX)
            dve.wait_ge(ident_high, 1)
            v.memset(den[:, :], 1.0).then_inc(tables_over, 1)

            def row_index(r, layer, signal):
                v.tensor_copy(idx[:, r.par, :], rows[:, layer, bass.ds(r.number, 1), :].rearrange("p j u -> p (j u)")
                              ).then_inc(signal[r.par], 1)

            def make_onehot(r, signal, to):
                d = dstl[:, bass.ds(r.number, 1), :].rearrange("p j u -> p (j u)").unsqueeze(2).broadcast_to([P, U, NODES])
                v.tensor_tensor(to[:, r.par, :, :], iota_n[:, :].unsqueeze(1).broadcast_to([P, U, NODES]), d,
                                ALU.is_equal).then_inc(signal, 1)

            def score(r, g):
                dve.wait_ge(kv_landed[r.par][g], r.loads(GU))
                for pr in range(2 * g, 2 * g + 2):
                    dve.wait_ge(qe_ready[pr % 2], r.nth(QB, pr // 2 + 1))
                    k = kv[:, r.par, 2 * pr:2 * pr + 2, 0:C]
                    ins = v.tensor_tensor(k, k, b_qe[pr % 2][:, :].rearrange("p (a c) -> p a c", a=2), ALU.mult)
                    ins.then_inc(qe_used[pr % 2], 1)
                for k in range(2):
                    dve.wait_ge(qe_used[k], r.nth(QB, g + 1))
                for u in range(g * GU, g * GU + GU, 4):
                    v.tensor_reduce(S[:, :, u:u + 4].rearrange("p h u -> p u h"),
                                    kv[:, r.par, u:u + 4, 0:C].rearrange("p u (h d) -> p u h d", h=H),
                                    AX.X, ALU.add).then_inc(scored, 1)

            def normalise(f, sums=b_agg):
                if sums is b_agg:
                    dve.wait_ge(agg_done, f.done)
                v.tensor_scalar_max(den[:NODES, :], sums[:NODES, C:C + H], 0.5).then_inc(den_ready, 1)
                dve.wait_ge(den_ready, f.done)
                v.reciprocal(rden[:NODES, :], den[:NODES, :]).then_inc(rden_ready, 1)
                dve.wait_ge(rden_ready, f.done)
                v.tensor_tensor(hN[:NODES, :].rearrange("p (h d) -> p h d", h=H),
                                sums[:NODES, 0:C].rearrange("p (h d) -> p h d", h=H),
                                rden[:NODES, :].unsqueeze(2).broadcast_to([NODES, H, D]), ALU.mult).then_inc(hN_ready, 1)
                dve.wait_ge(hN_ready, f.done)
                wait(dve, hT_filled[HALVES - 1], f.number)
                for t in range(NT):
                    last = v.tensor_scalar(hm[:NODES, t, :], hN[:NODES, :], calpha[:NODES, bass.ds(f.tile, 1), t],
                                           None, ALU.mult)
                last.then_inc(hm_ready, 1)

            def stats(f):
                dve.wait_ge(wa_done, f.done)
                dve.wait_ge(xs_ready, f.done)
                v.tensor_tensor(z[:NODES, :], z[:NODES, :], b_out[:NODES, 0:C], ALU.add).then_inc(z_ready, 1)
                dve.wait_ge(z_ready, f.done)
                v.bn_stats(st6[:NODES, :], z[:NODES, :]).then_inc(st_ready, 1)
                settle(dve, const_ready)
                dve.wait_ge(st_ready, f.done)
                v.bn_aggr(mv[:NODES, :], st6[:NODES, :]).then_inc(mv_ready, 1)

            def norm_rows(f):
                dve.wait_ge(sd_ready, f.done)
                v.reciprocal(rstd[:NODES, :], sd[:NODES, :]).then_inc(rstd_ready, 1)
                dve.wait_ge(rstd_ready, f.done)
                wait(dve, x1_stored, f.stores_before())
                v.tensor_scalar(x1[:NODES, f.par, :], z[:NODES, :], mv[:NODES, 0:1], rstd[:NODES, 0:1],
                                ALU.subtract, ALU.mult).then_inc(x1_ready, 1)

            def keep_x1T_low(f):
                dve.wait_ge(x1T_high, f.done)
                low_part(x1T_r[:, f.par, 1, :, :], b_x1T.rearrange("p (h n) -> p h n", h=HALVES),
                         x1T_r[:, f.par, 0, :, :]).then_inc(x1T_low, 1)

            def make_gates(f):
                dve.wait_ge(eg_ready, f.done)
                v.tensor_scalar_add(eg1[:NODES, :], eg[:NODES, :], 1.0).then_inc(eg1_ready, 1)
                dve.wait_ge(eg1_ready, f.done)
                v.reciprocal(gate[:NODES, f.par, :], eg1[:NODES, :]).then_inc(gate_ready, 1)

            def softmax(r):
                dve.wait_ge(scored, r.nth(G, G))
                dve.wait_ge(masks_ready, r.done)
                flat = lambda t: t.rearrange("p h u -> p (h u)")
                v.tensor_tensor_scan(flat(FB[:, 0, :, :]), flat(masks[:, 0, :, :]), flat(S[:, :, :]), -BIG, ALU.add, ALU.max)
                v.tensor_tensor_scan(flat(FB[:, 1, :, :])[:, ::-1], flat(masks[:, 1, :, :])[:, ::-1],
                                     flat(S[:, :, :])[:, ::-1], -BIG, ALU.add, ALU.max).then_inc(scanned, 1)

            def softmax_across(r):
                dve.wait_ge(carry_copied, r.done)
                v.tensor_tensor_scan(carry[:, 0, 1:P + 1], carry_in[:, 1, :], carry_in[:, 0, :], -BIG, ALU.add, ALU.max)
                v.tensor_tensor_scan(carry[:, 1, 0:P][:, ::-1], carry_in[:, 3, :][:, ::-1], carry_in[:, 2, :][:, ::-1],
                                     -BIG, ALU.add, ALU.max).then_inc(carried, 1)

            def softmax_less(r):
                dve.wait_ge(backT, r.done)
                pn = b_tmp[:, 0:2 * H].rearrange("p (k h) -> p k h", k=2).unsqueeze(3).broadcast_to([P, 2, H, U])
                re = reach[:, bass.ds(r.number, 1), :, :].rearrange("p j k u -> p (j k) u").unsqueeze(2).broadcast_to([P, 2, H, U])
                v.tensor_tensor(m2[:, :, :, :], pn, re, ALU.add).then_inc(m_a, 1)
                dve.wait_ge(m_a, r.done)
                v.tensor_tensor(m2[:, :, :, :], m2[:, :, :, :], FB[:, :, :, :], ALU.max).then_inc(m_b, 1)
                dve.wait_ge(m_b, r.done)
                v.tensor_tensor(m2[:, 0, :, :], m2[:, 0, :, :], m2[:, 1, :, :], ALU.max).then_inc(m_c, 1)
                dve.wait_ge(m_c, r.done)
                v.tensor_tensor(S[:, :, :], S[:, :, :], m2[:, 0, :, :], ALU.subtract).then_inc(d_ready, 1)

            def weigh(r):
                dve.wait_ge(ex_ready, r.done)
                for g in range(G):
                    u = slice(g * GU, g * GU + GU)
                    w = kv[:, r.par, u, C:2 * C].rearrange("p u (h d) -> p u h d", h=H)
                    e = kv[:, r.par, u, 2 * C:ROW].unsqueeze(3).broadcast_to([P, GU, H, D])
                    v.tensor_tensor(w, w, e, ALU.mult).then_inc(weighted[g], 1)

            def l0(r):
                f = None if r.first else r.last()
                score(r, 0)
                if r.older:
                    make_gates(r.older)
                score(r, 1)
                if f:
                    normalise(f)
                    if not r.final:
                        row_index(r.next(), 0, idx_ready)
                score(r, 2)
                score(r, 3)
                softmax(r)
                if f:
                    stats(f)
                if not r.final:
                    make_onehot(r.next(), oh_ready, onehot_r)
                softmax_across(r)
                if f:
                    norm_rows(f)
                softmax_less(r)
                weigh(r)
                if f:
                    keep_x1T_low(f)

            row_index(Round(dve, 0, 0), 0, idx_ready)
            row_index(Round(dve, 0, 1), 0, idx_ready)
            make_onehot(Round(dve, 0, 0), oh_ready, onehot_r)
            dve.wait_ge(carry_ends, 1)
            for h in range(HALVES):
                dve.wait_ge(wr_high, h + 1)
                low_part(wr_r[:, 1, h, :, :], wr[:, h, :, :], wr_r[:, 0, h, :, :]).then_inc(wr_low, 1)
            rounds(dve, l0)
            f = Round(dve, LAST, 1)
            make_gates(Round(dve, LAST, 0))
            normalise(f)
            stats(f)
            norm_rows(f)
            keep_x1T_low(f)
            make_gates(f)

            def finish(f, sums=None):
                wait(dve, l_y, f.number)
                if sums is None:
                    sums = bank[f.par]
                    dve.wait_ge(l_agg, f.done)
                dve.wait_ge(l_x[f.par], f.loads(1))
                v.scalar_tensor_tensor(z[:NODES, :], sums[:NODES, 0:C], 0.0, xb[:NODES, f.par, :],
                                       ALU.max, ALU.add).then_inc(l_z, 1)
                dve.wait_ge(l_z, f.done)
                v.bn_stats(st6[:NODES, :], z[:NODES, :]).then_inc(l_st, 1)
                settle(dve, const_ready)
                dve.wait_ge(l_st, f.done)
                v.bn_aggr(mv[:NODES, :], st6[:NODES, :]).then_inc(l_mv, 1)
                dve.wait_ge(l_sd, f.done)
                v.reciprocal(rstd[:NODES, :], sd[:NODES, :]).then_inc(l_rstd, 1)
                dve.wait_ge(l_rstd, f.done)
                wait(dve, l_out, f.stores_before())
                v.tensor_scalar(x1[:NODES, f.par, :], z[:NODES, :], mv[:NODES, 0:1], rstd[:NODES, 0:1],
                                ALU.subtract, ALU.mult).then_inc(l_y, 1)

            def l1(r):
                wait(dve, l_agg, r.before)
                make_onehot(r, l_oh0, onehot_w)
                dve.wait_ge(l_oh0, r.done)
                w = norms[:, bass.ds(r.number, 1), :].rearrange("p j u -> p (j u)").unsqueeze(2).broadcast_to([P, U, NODES])
                o = onehot_w[:, r.par, :, :]
                v.tensor_tensor(o, o, w, ALU.mult).then_inc(l_oh, 1)
                if not r.first:
                    finish(r.last())
                    if not r.final:
                        row_index(r.next(), 1, l_idx)

            row_index(Round(dve, 0, 0), 1, l_idx)
            row_index(Round(dve, 0, 1), 1, l_idx)
            dve.wait_ge(x1_stored, 16 * ROUNDS)
            dve.wait_ge(m_filled[1], ROUNDS * MB)
            rounds(dve, l1)
            finish(Round(dve, LAST, 1))

            with general(dve):
                def step_on(ins):
                    ins.then_inc(g_link, 1)
                    take(dve, g_link, 1)

                f = lambda k: g_rec_w[:, :, k]
                with dve.Fori(0, WINDOWS):
                    take(dve, g_in, 16)
                    v.scalar_tensor_tensor(idx[:, 0, :], f(0), float(ET), f(1), ALU.mult, ALU.add)
                    v.tensor_scalar(idx[:, 1, :], f(3), float(N - 1), None, ALU.min).then_inc(g_idx, 1)
                    take(dve, g_landed, 1)
                    q = kv[:, 1, :, 0:C]
                    step_on(v.tensor_tensor(q, q, kv[:, 1, :, C:2 * C], ALU.add))
                    step_on(v.tensor_tensor(q, q, kv[:, 0, :, 0:C], ALU.mult))
                    for u in range(0, U, GU):
                        ins = v.tensor_reduce(S[:, :, u:u + GU].rearrange("p h u -> p u h"),
                                              kv[:, 1, u:u + GU, 0:C].rearrange("p u (h d) -> p u h d", h=H),
                                              AX.X, ALU.add)
                    ins.then_inc(g_scored, 1)

                def segment_masks(at):
                    m = g_mask[:, at:at + RW]
                    step_on(v.tensor_tensor(m, g_here, g_beside, ALU.is_equal))
                    step_on(v.tensor_scalar(m, m, -1.0, BIG, ALU.add, ALU.mult))

                step_on(v.memset(g_val[:, 0:1], -BIG))
                step_on(v.memset(g_mask[:, 0:1], 0.0))
                with dve.Fori(0, WINDOWS):
                    take(dve, g_in, 3 * 16)
                    segment_masks(1)
                    step_on(v.tensor_tensor_scan(g_run, g_mask, g_val, -BIG, ALU.add, ALU.max))
                    v.tensor_copy(g_val[:, 0:1], g_run[:, RW:RW + 1]).then_inc(g_out, 1)
                step_on(v.memset(g_val[:, RW:RW + 1], -BIG))
                step_on(v.memset(g_mask[:, RW:RW + 1], 0.0))
                with dve.Fori(0, WINDOWS):
                    take(dve, g_in, 4 * 16)
                    segment_masks(0)
                    step_on(v.tensor_tensor_scan(g_run[:, ::-1], g_mask[:, ::-1], g_val[:, ::-1], -BIG, ALU.add, ALU.max))
                    step_on(v.tensor_copy(g_val[:, RW:RW + 1], g_run[:, 0:1]))
                    v.tensor_tensor(g_score, g_score, g_run[:, 0:RW], ALU.subtract).then_inc(g_less, 1)
                for h in range(HALVES):
                    dve.wait_ge(wr_high, HALVES + h + 1)
                    low_part(wr_r[:, 1, h, :, :], wr[:, h, :, :], wr_r[:, 0, h, :, :]).then_inc(wr_low, 1)

                def begin(tile, hot, field, types):
                    take(dve, g_in, 2 * 16)
                    v.scalar_tensor_tensor(idx[:, 0, :], f(0), float(types), f(field), ALU.mult, ALU.add).then_inc(g_idx, 1)
                    step_on(v.tensor_tensor(g_local, f(3), base[:, bass.ds(tile, 1)].broadcast_to([P, U]), ALU.subtract))
                    step_on(v.tensor_tensor(hot[:, 0, :, :], iota_n[:, :].unsqueeze(1).broadcast_to([P, U, NODES]),
                                            g_local.unsqueeze(2).broadcast_to([P, U, NODES]), ALU.is_equal))

                def add_window(width):
                    take(dve, g_summed, 1)
                    step_on(v.tensor_tensor(g_acc[:, 0:width], g_acc[:, 0:width], b_agg[:NODES, 0:width], ALU.add))
                    dve.sem_inc(g_next, 1)

                def tile0(r):
                    step_on(v.memset(g_acc, 0.0))
                    with dve.Fori(0, WINDOWS):
                        begin(r.tile, onehot_r, 1, ET)
                        take(dve, g_landed, 1)
                        step_on(v.tensor_copy(kv[:, 0, :, 2 * C:ROW], g_e.rearrange("p h u -> p u h")))
                        for g in range(G):
                            u = slice(g * GU, g * GU + GU)
                            w = kv[:, 0, u, C:2 * C].rearrange("p u (h d) -> p u h d", h=H)
                            e = kv[:, 0, u, 2 * C:ROW].unsqueeze(3).broadcast_to([P, GU, H, D])
                            ins = v.tensor_tensor(w, w, e, ALU.mult)
                        ins.then_inc(g_weighted, 1)
                        add_window(C + H)
                    normalise(r, g_acc)
                    stats(r)
                    norm_rows(r)
                    keep_x1T_low(r)
                    make_gates(r)
                tiles(dve, tile0)

                for b in range(PARTS):
                    dve.wait_ge(m_stored[b], 16 * (2 * ROUNDS + 1))
                dve.wait_ge(x1_stored, 2 * 16 * ROUNDS)
                dve.wait_ge(m_filled[1], 2 * ROUNDS * MB)

                def tile1(r):
                    step_on(v.memset(g_acc, 0.0))
                    with dve.Fori(0, WINDOWS):
                        begin(r.tile, onehot_w, 2, RT)
                        take(dve, g_landed, 1)
                        o = onehot_w[:, 0, :, :]
                        v.tensor_tensor(o, o, g_norm.unsqueeze(2).broadcast_to([P, U, NODES]), ALU.mult).then_inc(g_weighted, 1)
                        add_window(C)
                    finish(r, g_acc)
                tiles(dve, tile1)


def kernel(**inputs):
    import numpy as np
    import concourse.bacc as bacc
    from concourse.bass_utils import run_bass_kernel_spmd

    given = {k: np.asarray(v) for k, v in inputs.items()}
    x = np.zeros((NPAD, C), given["x"].dtype)
    x[:N] = given["x"]
    nt = np.zeros(NPAD, given["node_type_3"].dtype)
    nt[:N] = given["node_type_3"]
    dst = given["dst"]
    rec = np.zeros((EPAD, FIELDS), dst.dtype)
    for k, name in enumerate(("src", "edge_type_5", "edge_type_16")):
        rec[:E, k] = given[name]
    rec[:, 3:] = FAR
    rec[:E, 3] = dst
    rec[0, 4] = -1
    rec[1:E + 1, 4] = dst
    rec[:E - 1, 5] = dst[1:]
    norm = np.zeros(EPAD, given["edge_weight1"].dtype)
    norm[:E] = given["edge_weight1"][:, 0]
    grid = np.full(P * COUNT_COLS, FAR, dst.dtype)
    grid[:E] = dst
    arrays = {
        "x": x, "nt_rows": nt.reshape(TILES, NODES).T, "rec": rec, "dst_lines": rec[:, 3:].T, "norm": norm,
        "dst_grid": grid.reshape(P, COUNT_COLS),
        "Wk": given["L0_gnn_Wk"], "Wq": given["L0_gnn_Wq"], "Wv": given["L0_gnn_Wv"],
        "Ratt": given["L0_gnn_Ratt"], "Rmsg": given["L0_gnn_Rmsg"], "pri": given["L0_gnn_pri"].T,
        "Wa": given["L0_gnn_Wa"], "skip": given["L0_gnn_skip"], "Wr": given["L1_gnn_weight"],
        "gate_w": given["L1_gnn_gate_weight"][:, :, 0].T,
    }
    nc = bacc.Bacc("TRN2", target_bir_lowering=False, num_devices=1)
    sent, args = {}, {}
    for name, a in arrays.items():
        sent[f"in_{name}"] = np.ascontiguousarray(a)
        args[name] = nc.dram_tensor(f"in_{name}", a.shape, mybir.dt.from_np(a.dtype), kind="ExternalInput").ap()
    out = nc.dram_tensor("out", (ROUNDS * NODES, C), F32, kind="ExternalOutput").ap()
    build(nc, out=out, **args)
    result = run_bass_kernel_spmd(nc, [sent], core_ids=[0])
    return result.results[0]["out"][:N]
```
